# Optimizing a Trainium2 kernel written in Bass

```python
import numpy as np
import jax
import jax.numpy as jnp

def _softmax(x, axis=-1):
    return jax.nn.softmax(x, axis=axis)

def _gelu(x):
    return jax.nn.gelu(x, approximate=True)

def _silu(x):
    return jax.nn.silu(x)

def _sigmoid(x):
    return jax.nn.sigmoid(x)

def _layernorm(x, axis=-1, eps=1e-05):
    m = jnp.mean(x, axis=axis, keepdims=True)
    v = jnp.var(x, axis=axis, keepdims=True)
    return (x - m) / jnp.sqrt(v + eps)

def _scatter_add(tgt, idx, src, axis=0):
    return tgt.at[idx].add(src)

def _segment_sum(src, seg, n):
    return jax.ops.segment_sum(src, seg, n)
kernel_name = 'mk_adaln_ffn_d1_seqx_r4_d07a2f'

def setup_inputs(seed: int=0):
    np.random.seed(seed)
    _w = jnp.asarray

    def _rec_inputs():
        import jax
        import jax.numpy as jnp
        _rk = jax.random.key(seed)
        x = -0.0003929 + 0.9999 * jax.random.normal(jax.random.fold_in(_rk, 1), (64, 64, 1024), jnp.float32)
        _lenS = 64 - jax.random.randint(jax.random.fold_in(_rk, 7), (64,), 0, max(1, 64 // 4) + 1, jnp.int32)
        _lenS2 = 64 - jax.random.randint(jax.random.fold_in(_rk, 8), (64,), 0, max(1, 64 // 4) + 1, jnp.int32)
        cond_512 = 0.00782532 + 1.00527 * jax.random.normal(jax.random.fold_in(_rk, 11), (64, 128), jnp.float32)
        return (x, cond_512)
    x, cond_512 = _rec_inputs()

    def _L0_cond_setup():
        import jax, jax.numpy as jnp
        from jax import lax
        import numpy as np
        CIN, COUT, K, STYLE_DIM = (64, 64, 3, 128)
        N_LAYERS = 4
        TYPES = ('same', 'upsample', 'same', 'downsample')
        SCALE = 1.0 / float(np.sqrt(CIN * K ** 2))
        EPS = 1e-08
        _BK = np.array([1.0, 3.0, 3.0, 1.0], dtype=np.float32)
        BLUR_K = _BK / _BK.sum()

        def _blur(x, kern, pad):
            B, C, _ = x.shape
            xp = jnp.pad(x, ((0, 0), (0, 0), (pad[0], pad[1])))
            w = jnp.broadcast_to(kern.astype(x.dtype)[None, None, :], (C, 1, kern.shape[0]))
            return lax.conv_general_dilated(xp, w, (1,), 'VALID', feature_group_count=C, dimension_numbers=('NCH', 'OIH', 'NCH'))

        def _conv_same(x, w):
            p = (K - 1) // 2
            return lax.conv_general_dilated(x[None], w, (1,), [(p, p)], dimension_numbers=('NCH', 'OIH', 'NCH'))[0]

        def _conv_down(x, w):
            return lax.conv_general_dilated(x[None], w, (2,), 'VALID', dimension_numbers=('NCH', 'OIH', 'NCH'))[0]

        def _conv_up(x, w_t):
            return lax.conv_transpose(x[None], w_t, (2,), 'VALID', dimension_numbers=('NCH', 'IOH', 'NCH'), transpose_kernel=True)[0]

        def _layer(x, style, w, b, mw, mb, typ):
            s = style @ mw.T + mb
            weight = SCALE * w * s[:, None, :, None]
            demod = lax.rsqrt(jnp.sum(weight * weight, axis=(2, 3)) + EPS)
            weight = weight * demod[:, :, None, None]
            blur_k = jnp.asarray(BLUR_K)
            if typ == 'same':
                out = jax.vmap(_conv_same)(x, weight) + b[None, :, None]
            elif typ == 'upsample':
                out = jax.vmap(_conv_up)(x, weight.transpose(0, 2, 1, 3)) + b[None, :, None]
                out = _blur(out, 2.0 * blur_k, (1, 1))
            elif typ == 'downsample':
                xb = _blur(x, blur_k, (2, 2))
                out = jax.vmap(_conv_down)(xb, weight) + b[None, :, None]
            else:
                raise NotImplementedError(typ)
            return out
        key = jax.random.key(seed)
        ks = jax.random.split(key, 6)
        B, L = (16, 1024)
        return {'x': jax.random.normal(ks[0], (B, CIN, L), dtype=jnp.float32), 'style': jax.random.normal(ks[1], (B, STYLE_DIM), dtype=jnp.float32), 'weights': jax.random.normal(ks[2], (N_LAYERS, COUT, CIN, K), dtype=jnp.float32), 'biases': jax.random.normal(ks[3], (N_LAYERS, COUT), dtype=jnp.float32) * 0.1, 'mod_w': jax.random.normal(ks[4], (N_LAYERS, CIN, STYLE_DIM), dtype=jnp.float32) / np.sqrt(STYLE_DIM), 'mod_b': 1.0 + 0.1 * jax.random.normal(ks[5], (N_LAYERS, CIN), dtype=jnp.float32)}
    _L0_cond_all = _L0_cond_setup()
    _L0_cond_in = {k: v for k, v in _L0_cond_all.items() if k in ('weights', 'biases', 'mod_w', 'mod_b')}
    del _L0_cond_all

    def _L0_ffn_setup():
        import jax, jax.numpy as jnp
        import numpy as np
        NUM_EXPERTS = 4
        HIDDEN = 1024
        RANK = 8
        ALPHA = 8.0
        SCALE = ALPHA / RANK
        key = jax.random.key(seed)
        ks = jax.random.split(key, 6)
        B, T, H, E, R = (4, 1024, HIDDEN, NUM_EXPERTS, RANK)
        x = jax.random.normal(ks[0], (B, T, H), dtype=jnp.float32)
        W_up = jax.random.normal(ks[1], (H, H), dtype=jnp.float32) / np.sqrt(H)
        gate_w = jax.random.normal(ks[2], (E, H), dtype=jnp.float32) / np.sqrt(H)
        expert_bias = jnp.zeros((E,), dtype=jnp.float32)
        lora_A = jax.random.normal(ks[3], (E, R, H), dtype=jnp.float32) / np.sqrt(H)
        lora_B = jax.random.normal(ks[4], (E, H, R), dtype=jnp.float32) * 0.01
        return {'x': x, 'W_up': W_up, 'gate_w': gate_w, 'expert_bias': expert_bias, 'lora_A': lora_A, 'lora_B': lora_B}
    _L0_ffn_all = _L0_ffn_setup()
    _L0_ffn_in = {k: v for k, v in _L0_ffn_all.items() if k in ('W_up', 'gate_w', 'expert_bias', 'lora_A', 'lora_B')}
    del _L0_ffn_all
    return {'x': x, 'cond_512': cond_512, 'L0_cond_weights': _L0_cond_in['weights'], 'L0_cond_biases': _L0_cond_in['biases'], 'L0_cond_mod_w': _L0_cond_in['mod_w'], 'L0_cond_mod_b': _L0_cond_in['mod_b'], 'L0_ffn_W_up': _L0_ffn_in['W_up'], 'L0_ffn_gate_w': _L0_ffn_in['gate_w'], 'L0_ffn_expert_bias': _L0_ffn_in['expert_bias'], 'L0_ffn_lora_A': _L0_ffn_in['lora_A'], 'L0_ffn_lora_B': _L0_ffn_in['lora_B']}

def reference(x, cond_512, L0_cond_weights, L0_cond_biases, L0_cond_mod_w, L0_cond_mod_b, L0_ffn_W_up, L0_ffn_gate_w, L0_ffn_expert_bias, L0_ffn_lora_A, L0_ffn_lora_B):
    import jax
    import jax.numpy as jnp

    def _L0_cond_ref(x, style, weights, biases, mod_w, mod_b):
        import jax, jax.numpy as jnp
        from jax import lax
        import numpy as np
        CIN, COUT, K, STYLE_DIM = (64, 64, 3, 128)
        N_LAYERS = 4
        TYPES = ('same', 'upsample', 'same', 'downsample')
        SCALE = 1.0 / float(np.sqrt(CIN * K ** 2))
        EPS = 1e-08
        _BK = np.array([1.0, 3.0, 3.0, 1.0], dtype=np.float32)
        BLUR_K = _BK / _BK.sum()

        def _blur(x, kern, pad):
            B, C, _ = x.shape
            xp = jnp.pad(x, ((0, 0), (0, 0), (pad[0], pad[1])))
            w = jnp.broadcast_to(kern.astype(x.dtype)[None, None, :], (C, 1, kern.shape[0]))
            return lax.conv_general_dilated(xp, w, (1,), 'VALID', feature_group_count=C, dimension_numbers=('NCH', 'OIH', 'NCH'))

        def _conv_same(x, w):
            p = (K - 1) // 2
            return lax.conv_general_dilated(x[None], w, (1,), [(p, p)], dimension_numbers=('NCH', 'OIH', 'NCH'))[0]

        def _conv_down(x, w):
            return lax.conv_general_dilated(x[None], w, (2,), 'VALID', dimension_numbers=('NCH', 'OIH', 'NCH'))[0]

        def _conv_up(x, w_t):
            return lax.conv_transpose(x[None], w_t, (2,), 'VALID', dimension_numbers=('NCH', 'IOH', 'NCH'), transpose_kernel=True)[0]

        def _layer(x, style, w, b, mw, mb, typ):
            s = style @ mw.T + mb
            weight = SCALE * w * s[:, None, :, None]
            demod = lax.rsqrt(jnp.sum(weight * weight, axis=(2, 3)) + EPS)
            weight = weight * demod[:, :, None, None]
            blur_k = jnp.asarray(BLUR_K)
            if typ == 'same':
                out = jax.vmap(_conv_same)(x, weight) + b[None, :, None]
            elif typ == 'upsample':
                out = jax.vmap(_conv_up)(x, weight.transpose(0, 2, 1, 3)) + b[None, :, None]
                out = _blur(out, 2.0 * blur_k, (1, 1))
            elif typ == 'downsample':
                xb = _blur(x, blur_k, (2, 2))
                out = jax.vmap(_conv_down)(xb, weight) + b[None, :, None]
            else:
                raise NotImplementedError(typ)
            return out
        out = x
        for i, typ in enumerate(TYPES):
            out = _layer(out, style, weights[i], biases[i], mod_w[i], mod_b[i], typ)
        return out

    def _L0_ffn_ref(x, W_up, gate_w, expert_bias, lora_A, lora_B):
        import jax, jax.numpy as jnp
        import numpy as np
        NUM_EXPERTS = 4
        HIDDEN = 1024
        RANK = 8
        ALPHA = 8.0
        SCALE = ALPHA / RANK
        B, T, H = x.shape
        E = gate_w.shape[0]
        x_flat = x.reshape(-1, H)
        logits = x_flat @ gate_w.T + expert_bias
        top1 = jnp.argmax(logits, axis=-1)
        one_hot = jax.nn.one_hot(top1, E, dtype=x_flat.dtype)
        base_out = jnp.einsum('bth,oh->bto', x, W_up)
        z = jnp.einsum('nh,erh->ner', x_flat, lora_A)
        d = jnp.einsum('ner,ehr->neh', z, lora_B) * SCALE
        delta = jnp.einsum('neh,ne->nh', d, one_hot)
        return base_out + delta.reshape(B, T, H)
    x = x + _L0_ffn_ref(_L0_cond_ref(x, cond_512, L0_cond_weights, L0_cond_biases, L0_cond_mod_w, L0_cond_mod_b), L0_ffn_W_up, L0_ffn_gate_w, L0_ffn_expert_bias, L0_ffn_lora_A, L0_ffn_lora_B)
    return x

_drawn_inputs = setup_inputs


def setup_inputs(seed=0):
    import zlib

    import numpy as np

    out = dict(_drawn_inputs(seed))
    spreads = {'L0_ffn_expert_bias': (0.0, 0.8)}
    factors = {'L0_ffn_gate_w': 4.06, 'L0_ffn_lora_A': 3.554, 'L0_ffn_lora_B': 3.559}
    for name, (base, spread) in spreads.items():
        noise = np.random.default_rng([zlib.crc32(name.encode()), seed]).standard_normal(out[name].shape)
        drawn = base * np.exp(spread * noise) if base else spread * noise
        out[name] = jnp.asarray(drawn.astype(out[name].dtype))
    for name, factor in factors.items():
        out[name] = (out[name] * factor).astype(out[name].dtype)
    return out
```

```python
from contextlib import ExitStack

import concourse.bass as bass
from concourse import mybir

F32 = mybir.dt.float32
F32R = mybir.dt.float32r
ALU = mybir.AluOpType
ACT = mybir.ActivationFunctionType
AX_X = mybir.AxisListType.X

P = 128
HI, LO = 0, 1


def adaln_ffn_kernel(
    nc: bass.Bass,
    x: bass.AP,
    cond: bass.AP,
    conv_w: bass.AP,
    conv_b: bass.AP,
    mod_w: bass.AP,
    mod_b: bass.AP,
    W_up: bass.AP,
    gate_w: bass.AP,
    expert_bias: bass.AP,
    lora_A: bass.AP,
    lora_B: bass.AP,
    out: bass.AP,
):
    B, C, T = x.shape
    L, _, _, K = conv_w.shape
    D = cond.shape[1]
    E = gate_w.shape[0]
    R = lora_A.shape[1]
    ER = E * R
    PAIRS = B // 2
    S = T // 2
    SB = S // P
    CH = 2 * SB
    GA = E + ER
    NW = GA + T
    SCALE = float(1.0 / (C * K) ** 0.5)
    EPS = 1e-8
    BLUR = [0.125, 0.375, 0.375, 0.125]
    M = 6
    HB = T // P
    REG = [(0, 354), (354, 354), (708, 352)]
    assert C == 64 and P == 2 * C and T == 1024 and D == P and L == 4 and K == 3 and NW == 1060
    EDGES = 2
    last = PAIRS - 1

    ctx = ExitStack()
    with ctx:
        def sb(name, shape, dt=F32):
            return ctx.enter_context(nc.sbuf_tensor(name, shape, dt))

        def pb(name):
            return ctx.enter_context(nc.psum_tensor(name, [P, 512], F32))

        def sem(name):
            return ctx.enter_context(nc.semaphore(name))

        ga_nat = sb("ga_nat", [GA, T])
        lb_nat = sb("lb_nat", [P, HB, E, R])
        ebias = sb("ebias", [P, E])
        ident = sb("ident", [P, P])
        smallT = sb("smallT", [P, 2 * L])
        d_all = sb("d_all", [P, L, B])
        s0 = sb("s0", [P, B])
        E1 = sb("E1", [P, B])
        E2 = sb("E2", [P, B])
        E3 = sb("E3", [P, B])
        b0d = sb("b0d", [P, B])
        lb3 = sb("lb3", [P, HB, 3, ER], F32R)
        h_col = sb("h_col", [P, 2, 2, B], F32R)
        y_fix = sb("y_fix", [P, 3, B])
        stat = sb("stat", [P, 2, 7, P], F32R)
        t_const = sb("t_const", [P, 4, C])
        with ExitStack() as setup:
            def tmp(name, shape, dt=F32):
                return setup.enter_context(nc.sbuf_tensor(name, shape, dt))

            w_nat = tmp("w_nat", [P, L, C * K])
            modw_nat = tmp("modw_nat", [P, 2, D])
            cond_nat = tmp("cond_nat", [C, D])
            small = tmp("small", [2 * L, P])
            x_edge = tmp("x_edge", [C, EDGES, B, 6])
            condT = tmp("condT", [D, B])
            modwT = tmp("modwT", [D, L, 2, C])
            s_all = tmp("s_all", [P, L, B])
            s_sq = tmp("s_sq", [P, L, B])
            var = tmp("var", [P, L, B])
            rt_tmp = tmp("rt_tmp", [P, L, B])
            w_sq = tmp("w_sq", [P, L * C * K])
            w2_sum = tmp("w2_sum", [P, L, C])
            w2_sumT = tmp("w2_sumT", [C, L, P])
            w_dup = tmp("w_dup", [P, L * K, 2, C])
            wT = tmp("wT", [P, L * K, P])
            V1T = tmp("V1T", [P, M, P])
            V3T = tmp("V3T", [P, M, P])
            V1n = tmp("V1n", [C, M, C])
            stat32 = tmp("stat32", [P, 7, P])
            v_tab = tmp("v_tab", [P, 3, P])
            y_tab = tmp("y_tab", [P, 4, P])
            s2 = tmp("s2", [P, B])
            s3 = tmp("s3", [P, B])
            u_bias = tmp("u_bias", [P, B])
            u_bias8 = tmp("u_bias8", [P, B])
            v_bias = tmp("v_bias", [P, B])
            xs_edge = tmp("xs_edge", [C, EDGES, 7, B])
            h_raw = tmp("h_raw", [P, EDGES, 5, B])
            h_edge_s = tmp("h_edge_s", [C, EDGES, 6, B])
            u_edge = tmp("u_edge", [P, EDGES, 5, B])
            v_edge = tmp("v_edge", [P, EDGES, 4, B])
            v_int = tmp("v_int", [P, B])
        WT = sb("WT", [P, 2, CH, NW], F32R)
        BT = sb("BT", [3 * ER, T], F32R)
        first_w = sb("first_w", [P, E])
        X = sb("X", [P, 2, 2, T + 2])
        XS = sb("XS", [P, 2, 2, S + 2], F32R)
        H = sb("H", [P, 2, 2, S + 4], F32R)
        TT = sb("TT", [P, 2, 2, 4 * C], F32R)
        Q = sb("Q", [P, 2, 2, 5 * C], F32R)
        RR = sb("RR", [P, 2, 2, 8 * C], F32R)
        Y = sb("Y", [P, 2, S])
        YT = sb("YT", [P, 2, 2, CH, P], F32R)
        rows = sb("rows", [P, 4, T])
        OUT, XR = rows[:, 0:2, :], rows[:, 2:4, :]
        wup_nat = rows
        lg = sb("lg", [P, E])
        lg_max = sb("lg_max", [P, 1])
        sc = sb("sc", [P, E])
        sc_max = sb("sc_max", [P, 1])
        zm = sb("zm", [P, ER])
        zm3 = sb("zm3", [P, 3, ER], F32R)
        zT = sb("zT", [3 * ER, P], F32R)

        hB, qB, rB, yB, tB = pb("hB"), pb("qB"), pb("rB"), pb("yB"), pb("tB")
        fB = [pb("zB"), pb("f1B"), pb("f2B")]
        wtB = [tB, rB, yB]

        l_mod = sem("l_mod")
        l_w = sem("l_w")
        l_edge = sem("l_edge")
        l_wup = [sem(f"l_wup{n}") for n in range(4)]
        l_ga = sem("l_ga")
        l_lb = sem("l_lb")
        ident_ready = sem("ident_ready")
        pool_zero = sem("pool_zero")
        dve_setup = sem("dve_setup")
        dve_zero = sem("dve_zero")
        modT_psum = sem("modT_psum")
        modT_ready = sem("modT_ready")
        s_psum = sem("s_psum")
        s_ready = sem("s_ready")
        w2_ready = sem("w2_ready")
        w2T_psum = sem("w2T_psum")
        w2T_ready = sem("w2T_ready")
        wdup_ready = sem("wdup_ready")
        wT_psum = sem("wT_psum")
        wT_ready = sem("wT_ready")
        d_psum = sem("d_psum")
        var_ready = sem("var_ready")
        root_ready = sem("root_ready")
        scales_ready = sem("scales_ready")
        tables_ready = sem("tables_ready")
        xs_edge_ready = sem("xs_edge_ready")
        he_psum = sem("he_psum")
        he_ready = sem("he_ready")
        ue_psum = sem("ue_psum")
        ue_ready = sem("ue_ready")
        ve_psum = sem("ve_psum")
        ve_ready = sem("ve_ready")
        ye_psum = sem("ye_psum")
        edges_ready = sem("edges_ready")
        etab_ready = sem("etab_ready")
        lb3_ready = sem("lb3_ready")
        wt_psum = sem("wt_psum")
        wt_hi = sem("wt_hi")
        wt_lo = sem("wt_lo")
        x_landed = [sem(f"x_landed{p}") for p in range(2)]
        xr_landed = [sem(f"xr_landed{p}") for p in range(2)]
        out_stored = [sem(f"out_stored{p}") for p in range(2)]
        xs_hi, xs_lo = sem("xs_hi"), sem("xs_lo")
        t_hi, t_lo = sem("t_hi"), sem("t_lo")
        h_psum, h_hi, h_lo, h_cols = sem("h_psum"), sem("h_hi"), sem("h_lo"), sem("h_cols")
        q_psum, q_hi, q_lo = sem("q_psum"), sem("q_hi"), sem("q_lo")
        r_psum, r_hi, r_lo = sem("r_psum"), sem("r_hi"), sem("r_lo")
        y_psum, y_mid, y_cols = sem("y_psum"), sem("y_mid"), sem("y_cols")
        yt_psum, yt_hi, yt_lo = sem("yt_psum"), sem("yt_hi"), sem("yt_lo")
        z_psum = sem("z_psum")
        z_chain = sem("z_chain")
        zm_ready = sem("zm_ready")
        zt_psum = sem("zt_psum")
        zt_ready = sem("zt_ready")
        f_psum = sem("f_psum")
        added = sem("added")

        N_WT = 2 * HB + 1 + 2

        def upto(i, a):
            return i * 2 + (a + 1)

        def col(tab, i, a):
            return tab[:, bass.ds(i * 2 + a, 1)]

        x_conv = x.rearrange("(i a) c t -> i c a t", a=2)
        x_rows = x.rearrange("(i a) c t -> i (a c) t", a=2)
        out_rows = out.rearrange("(i a) c t -> i (a c) t", a=2)

        block = ctx.enter_context(nc.Block())

        @block.sync
        def _(sp):
            sp.dma_start(cond_nat[:], cond).then_inc(l_mod, 16)
            sp.dma_start(modw_nat[:], mod_w.rearrange("i c d -> (i c) d").rearrange("(g p) d -> p g d", p=P)).then_inc(l_mod, 16)
            for n, rows in enumerate((mod_b, conv_b)):
                for half in range(2):
                    sp.dma_start(small[L * n:L * n + L, C * half:C * half + C], rows).then_inc(l_mod, 16)
            for half in range(2):
                sp.dma_start(w_nat[C * half:C * half + C, :, :],
                             conv_w.rearrange("i o c k -> o i (c k)")).then_inc(l_w, 16)

            def load_x(i, par):
                sp.dma_start(X[0:C, par, :, 2:T + 2], x_conv[i]).then_inc(x_landed[par], 16)
                sp.dma_start(X[C:P, par, :, 1:T + 1], x_conv[i]).then_inc(x_landed[par], 16)

            load_x(0, 0)
            sp.dma_start(x_edge[:, 0, :, :], x[:, :, 0:6].rearrange("b c t -> c b t")).then_inc(l_edge, 16)
            sp.dma_start(x_edge[:, 1, :, :], x[:, :, T - 6:T].rearrange("b c t -> c b t")).then_inc(l_edge, 16)
            for n in range(4):
                sp.dma_start(wup_nat[:, n, :], W_up[P * n:P * n + P, :]).then_inc(l_wup[n], 16)
            load_x(1, 1)
            sp.dma_start(ebias[:], expert_bias.partition_broadcast(P)).then_inc(l_ga, 16)
            sp.dma_start(ga_nat[0:E, :], gate_w).then_inc(l_ga, 16)
            sp.dma_start(ga_nat[E:GA, :], lora_A.rearrange("e r h -> (e r) h")).then_inc(l_ga, 16)
            for e in range(E):
                sp.dma_start(lb_nat[:, :, e, :], lora_B[e].rearrange("(g p) r -> p g r", p=P)).then_inc(l_lb, 16)
            for n in range(4, HB):
                sp.wait_ge(wt_psum, 2 * (n - 3))
                sp.dma_start(wup_nat[:, n % 4, :], W_up[P * n:P * n + P, :]).then_inc(l_wup[n % 4], 16)

            def step(i, par, load=True, xr=True, store=True):
                if xr:
                    if not isinstance(i, int) or i >= 2:
                        sp.wait_ge(added, i * 3 - 3)
                    sp.dma_start(XR[:, par, :], x_rows[i]).then_inc(xr_landed[par], 16)
                if load:
                    sp.wait_ge(xs_lo, upto(i, 1))
                    load_x(i + 2, par)
                if store:
                    sp.wait_ge(added, i * 3)
                    sp.dma_start(out_rows[i - 1], OUT[:, 1 - par, :]).then_inc(out_stored[1 - par], 16)

            sp.wait_ge(wt_psum, 2 * HB)
            step(0, 0, store=False)
            step(1, 1)
            with sp.Fori(0, (PAIRS - 4) // 2) as k:
                step(k * 2 + 2, 0)
                step(k * 2 + 3, 1)
            step(PAIRS - 2, 0, load=False)
            step(PAIRS - 1, 1, load=False)
            step(PAIRS, 0, load=False, xr=False)
            for par in range(2):
                sp.wait_ge(out_stored[par], 16 * (PAIRS // 2))

        @block.gpsimd
        def _(pool):
            nc.gpsimd.memset(ident[:], 0.0).then_inc(pool_zero, 1)
            pool.wait_ge(pool_zero, 1)
            nc.gpsimd.affine_select(out=ident[:], in_=ident[:], compare_op=ALU.not_equal, fill=1.0,
                                    base=0, pattern=[[-1, P]], channel_multiplier=1).then_inc(ident_ready, 1)
            nc.gpsimd.memset(v_tab[:], 0.0)
            nc.gpsimd.memset(y_tab[:], 0.0)
            nc.gpsimd.memset(t_const[:], 0.0)
            nc.gpsimd.memset(u_edge[:], 0.0)
            nc.gpsimd.memset(v_edge[:], 0.0)
            nc.gpsimd.memset(h_edge_s[:], 0.0)
            nc.gpsimd.memset(xs_edge[:], 0.0)
            for e in range(E):
                nc.gpsimd.memset(first_w[:, e:e + 1], float(E - e))
            nc.gpsimd.memset(X[:, :, :, 0:1], 0.0).then_inc(pool_zero, 1)
            pool.wait_ge(pool_zero, 2)
            pool.wait_ge(edges_ready, 1)

            def step(i, first=False):
                for a in range(2):
                    if not first:
                        pool.wait_ge(y_psum, upto(i, a) - 2)
                    nc.gpsimd.tensor_copy(H[:, a, :, 1:S + 2:S].unsqueeze(3),
                                          h_col[:, :, :, bass.ds(i * 2 + a, 1)]).then_inc(h_cols, 1)
                    if not first:
                        pool.wait_ge(yt_psum, upto(i, a) - 2)
                    nc.gpsimd.tensor_copy(Y[:, a, 0:S:S - 1].unsqueeze(2),
                                          y_fix[:, 0:2, bass.ds(i * 2 + a, 1)]).then_inc(y_cols, 1)

            step(0, first=True)
            with pool.Fori(1, PAIRS) as i:
                step(i)

        @block.scalar
        def _(act):
            act.wait_ge(var_ready, 1)
            nc.scalar.activation(rt_tmp[:], var[:], ACT.Sqrt).then_inc(root_ready, 1)
            act.wait_ge(pool_zero, 2)
            act.wait_ge(tables_ready, 2)
            nc.scalar.activation(stat[:, HI, :, :], stat32[:], ACT.Copy).then_inc(root_ready, 1)
            T2 = 2 * K
            for rows, c0, tab, tap in ((0, 0, 0, 1), (0, C, 0, 0), (C, 0, 0, 2), (C, C, 0, 1),
                                       (C, 0, 1, 0), (0, C, 2, 2)):
                nc.scalar.activation(v_tab[rows:rows + C, tab, c0:c0 + C], wT[rows:rows + C, T2 + tap, c0:c0 + C], ACT.Copy)
            for e in range(2):
                r = slice(C * e, C * e + C)
                nc.scalar.activation(y_tab[r, 0:3, 0:C], V3T[r, e::2, 0:C], ACT.Copy)
                tail = nc.scalar.activation(y_tab[r, 1:4, C:P], V3T[r, e::2, C:P], ACT.Copy)
            tail.then_inc(etab_ready, 1)
            act.wait_ge(scales_ready, 1)

            def split_x(i, a, par, k, first=False):
                if a == 0:
                    act.wait_ge(x_landed[par], k * 32 + 32)
                if not first:
                    act.wait_ge(h_psum, upto(i, a) - 2)
                nc.scalar.activation(XS[:, a, HI, 0:S + 1], X[:, par, a, 0:T + 1:2], ACT.Copy,
                                     scale=col(s0, i, a)).then_inc(xs_hi, 1)

            def scale_t(i, a, first=False):
                if not first:
                    act.wait_ge(q_psum, upto(i, a) - 2)
                nc.scalar.activation(TT[:, a, HI, :], t_const[:], ACT.Copy, scale=col(E3, i, a)).then_inc(t_hi, 1)

            def conv_out(i, a, first=False):
                act.wait_ge(h_psum, upto(i, a))
                if not first:
                    act.wait_ge(y_psum, upto(i, a) - 2)
                nc.scalar.activation(H[:, a, HI, 2:S + 1], hB[:, 1:S], ACT.Identity,
                                     bias=col(b0d, i, a)).then_inc(h_hi, 1)
                act.wait_ge(q_psum, upto(i, a))
                if not first:
                    act.wait_ge(r_psum, upto(i, a) - 2)
                nc.scalar.activation(Q[:, a, HI, :], qB[:, 0:5 * C], ACT.Copy, scale=col(E2, i, a)).then_inc(q_hi, 1)

            def r_out(i, a):
                act.wait_ge(r_psum, upto(i, a))
                nc.scalar.activation(RR[0:C, a, HI, 0:7 * C], rB[0:C, 0:7 * C], ACT.Copy,
                                     scale=E1[0:C, bass.ds(i * 2 + a, 1)])
                nc.scalar.activation(RR[C:P, a, HI, C:8 * C], rB[C:P, 0:7 * C], ACT.Copy,
                                     scale=E1[C:P, bass.ds(i * 2 + a, 1)]).then_inc(r_hi, 1)

            def y_out(i, a, first=False):
                act.wait_ge(y_psum, upto(i, a))
                if not first:
                    act.wait_ge(yt_psum, upto(i, a) - 2)
                nc.scalar.activation(Y[:, a, 1:S - 1], yB[:, 1:S - 1], ACT.Identity,
                                     scale=d_all[:, 3, bass.ds(i * 2 + a, 1)],
                                     bias=y_fix[:, 2, bass.ds(i * 2 + a, 1)]).then_inc(y_mid, 1)

            def yt_out(i, a, par, wait=True):
                act.wait_ge(yt_psum, upto(i, a))
                if wait:
                    act.wait_ge(f_psum, i * 3 - 3)
                nc.scalar.activation(YT[:, par, HI, :, C * a:C * a + C],
                                     tB[:, :].rearrange("p (c o) -> p c o", o=C), ACT.Copy).then_inc(yt_hi, 1)

            def step(i, par, k, conv=True, ffn=True, ahead=True, first=False):
                early = first or (isinstance(i, int) and i < 2)
                if ffn:
                    yt_out(i - 1, 1, 1 - par, wait=not (isinstance(i, int) and i == 1) and True)
                if conv:
                    for a in range(2):
                        conv_out(i, a, first=first)
                        if ahead:
                            split_x(i + 1, a, 1 - par, k + par)
                            scale_t(i + 1, a)
                        r_out(i, a)
                    y_out(i, 0, first=first)
                if ffn:
                    act.wait_ge(zt_psum, i)
                    nc.scalar.activation(zT[:], tB[0:3 * ER, 0:P], ACT.Copy).then_inc(zt_ready, 1)
                if conv:
                    yt_out(i, 0, par, wait=not early)
                    y_out(i, 1, first=first)

            for a in range(2):
                split_x(0, a, 0, 0, first=True)
                scale_t(0, a, first=True)
            act.wait_ge(edges_ready, 1)
            step(0, 0, 0, ffn=False, first=True)
            for n in range(N_WT):
                act.wait_ge(wt_psum, n + 1)
                if n < 2 * HB:
                    c0, ob = CH // 2 * (n % 2), n // 2
                    nc.scalar.activation(WT[:, HI, c0:c0 + CH // 2, GA + P * ob:GA + P * ob + P],
                                         fB[n % 3][:, :].rearrange("p (c o) -> p c o", o=P), ACT.Copy).then_inc(wt_hi, 1)
                elif n == 2 * HB:
                    nc.scalar.activation(WT[:, HI, :, 0:GA],
                                         fB[n % 3][:, 0:CH * GA].rearrange("p (c o) -> p c o", o=GA),
                                         ACT.Copy).then_inc(wt_hi, 1)
                else:
                    h0 = 512 * (n - 2 * HB - 1)
                    nc.scalar.activation(BT[:, h0:h0 + 512], fB[n % 3][0:3 * ER, :], ACT.Copy).then_inc(wt_hi, 1)
            step(1, 1, 0)
            with act.Fori(0, (PAIRS - 4) // 2) as k:
                step(k * 2 + 2, 0, k + 1)
                step(k * 2 + 3, 1, k + 1)
            step(PAIRS - 2, 0, PAIRS // 2 - 1)
            step(PAIRS - 1, 1, PAIRS // 2 - 1, ahead=False)
            step(PAIRS, 0, PAIRS // 2, conv=False)

        @block.vector
        def _(dve):
            done = [0]

            def link(ins):
                done[0] += 1
                ins.then_inc(dve_setup, 1)
                dve.wait_ge(dve_setup, done[0])

            nc.vector.memset(stat32[:], 0.0)
            nc.vector.memset(V1T[:], 0.0)
            nc.vector.memset(V3T[:], 0.0)
            nc.vector.memset(V1n[:], 0.0)
            nc.vector.memset(H[:].bitcast(F32), 0.0)
            nc.vector.memset(h_col[:].bitcast(F32), 0.0)
            link(nc.vector.memset(RR[:].bitcast(F32), 0.0))
            dve.wait_ge(l_w, 32)
            wv = w_nat[:, :, :].rearrange("p i (c k) -> p i k c", k=K)
            for i in range(L):
                for half in range(2):
                    ins = nc.vector.tensor_copy(w_dup[:, K * i:K * i + K, half, :], wv[:, i, :, :])
            ins.then_inc(wdup_ready, 1)
            flat = w_nat[:, :, :].rearrange("p i n -> p (i n)")
            link(nc.vector.tensor_tensor(w_sq[:], flat, flat, ALU.mult))
            nc.vector.tensor_reduce(w2_sum[:, :, :].rearrange("p i c -> p (i c)"),
                                    w_sq[:, :].rearrange("p (n k) -> p n k", k=K), AX_X, ALU.add).then_inc(w2_ready, 1)
            dve.wait_ge(modT_psum, 1)
            nc.vector.tensor_copy(condT[:], qB[:, 0:B])
            nc.vector.tensor_copy(smallT[:], qB[:, B:B + 2 * L])
            for half in range(2):
                ins = nc.vector.tensor_copy(modwT[:, :, half, :], qB[:, P:P + L * C].rearrange("p (i c) -> p i c", c=C))
            ins.then_inc(modT_ready, 1)
            dve.wait_ge(modT_ready, 1)
            dve.wait_ge(w2T_psum, 1)
            nc.vector.tensor_copy(w2_sumT[:], hB[0:C, :].rearrange("p (i o) -> p i o", o=P)).then_inc(w2T_ready, 1)
            dve.wait_ge(s_psum, 1)
            for i in range(L):
                ins = nc.vector.tensor_scalar(s_all[:, i, :], rB[:, B * i:B * i + B], smallT[:, i:i + 1], None, ALU.add)
            link(ins)
            nc.vector.tensor_tensor(s_sq[:], s_all[:], s_all[:], ALU.mult).then_inc(s_ready, 1)
            dve.wait_ge(d_psum, 1)
            nc.vector.tensor_scalar(var[:], yB[:, 0:L * B].rearrange("p (i b) -> p i b", b=B),
                                    SCALE * SCALE, EPS, ALU.mult, ALU.add).then_inc(var_ready, 1)
            for n in range(3):
                dve.wait_ge(wT_psum, n + 1)
                nc.vector.tensor_copy(wT[:, 4 * n:4 * n + 4, :],
                                      fB[n][:, :].rearrange("p (t o) -> p t o", o=P)).then_inc(wT_ready, 1)
            dve.wait_ge(wT_ready, 3)
            for j in range(4):
                nc.vector.scalar_tensor_tensor(V1n[:, 3 - j:6 - j, :], w_dup[0:C, K:2 * K, 0, :], 2 * BLUR[j],
                                               V1n[:, 3 - j:6 - j, :], ALU.mult, ALU.add)
                nc.vector.scalar_tensor_tensor(V1T[:, 3 - j:6 - j, :], wT[:, K:2 * K, :], 2 * BLUR[j],
                                               V1T[:, 3 - j:6 - j, :], ALU.mult, ALU.add)
                link(nc.vector.scalar_tensor_tensor(V3T[:, j:j + 3, :], wT[:, 3 * K:4 * K, :], BLUR[j],
                                                    V3T[:, j:j + 3, :], ALU.mult, ALU.add))
            nc.vector.tensor_scalar(v_bias[:, 0:1], V3T[:, 0, 0:1], 0.0, None, ALU.mult).then_inc(tables_ready, 1)
            dve.wait_ge(root_ready, 1)
            link(nc.vector.reciprocal(d_all[:], rt_tmp[:]))
            link(nc.vector.tensor_tensor(rt_tmp[:], d_all[:], d_all[:], ALU.mult))
            link(nc.vector.tensor_tensor(rt_tmp[:], rt_tmp[:], var[:], ALU.mult))
            link(nc.vector.tensor_scalar(rt_tmp[:], rt_tmp[:], -0.5, 1.5, ALU.mult, ALU.add))
            link(nc.vector.tensor_tensor(d_all[:], d_all[:], rt_tmp[:], ALU.mult))
            nc.vector.tensor_scalar(s0[:], s_all[:, 0, :], SCALE, None, ALU.mult)
            nc.vector.tensor_scalar(s2[:], s_all[:, 2, :], SCALE, None, ALU.mult)
            nc.vector.tensor_scalar(s3[:], s_all[:, 3, :], SCALE, None, ALU.mult)
            nc.vector.scalar_tensor_tensor(E1[:], d_all[:, 0, :], SCALE, d_all[:, 1, :], ALU.mult, ALU.mult)
            link(nc.vector.tensor_tensor(b0d[:], var[:, 0, :], d_all[:, 0, :], ALU.mult))
            nc.vector.tensor_tensor(E2[:], s2[:], s_all[:, 1, :], ALU.mult)
            nc.vector.tensor_tensor(E3[:], s3[:], d_all[:, 2, :], ALU.mult)
            nc.vector.tensor_scalar(u_bias[:], s2[:], smallT[:, L + 1:L + 2], 2.0, ALU.mult, ALU.mult)
            nc.vector.tensor_scalar(v_bias[:], s3[:], smallT[:, L + 2:L + 3], None, ALU.mult)
            link(nc.vector.tensor_scalar(b0d[:], b0d[:], smallT[:, L:L + 1], None, ALU.mult))
            nc.vector.tensor_scalar(u_bias8[:], u_bias[:], BLUR[0], None, ALU.mult).then_inc(scales_ready, 1)
            dve.wait_ge(pool_zero, 2)
            for w in range(3):
                nc.vector.tensor_copy(t_const[0:C, w, :], V3T[0:C, 5 - 2 * w, 0:C])
                nc.vector.tensor_copy(t_const[C:P, w + 1, :], V3T[C:P, 4 - 2 * w, 0:C])
            T0, T2 = 0, 2 * K
            for rows, c0, tab, tap in ((0, 0, 0, 0), (C, 0, 0, 1), (C, C, 0, 0),
                                       (0, 0, 1, 2), (0, C, 1, 1), (C, C, 1, 2)):
                nc.vector.tensor_copy(stat32[rows:rows + C, tab, c0:c0 + C], wT[rows:rows + C, T0 + tap, c0:c0 + C])
            for rows, c0, tab, tap in ((0, 0, 2, 2), (C, 0, 2, 1), (C, C, 2, 2),
                                       (0, 0, 3, 0), (0, C, 3, 1), (C, C, 3, 0)):
                nc.vector.tensor_copy(stat32[rows:rows + C, tab, c0:c0 + C], w_dup[rows:rows + C, T2 + tap, 0, :])
            for e in range(2):
                r = slice(C * e, C * e + C)
                ins = nc.vector.tensor_copy(stat32[r, 4:7, :], V1T[r, e::2, :])
            ins.then_inc(tables_ready, 1)
            dve.wait_ge(tables_ready, 2)
            dve.wait_ge(root_ready, 2)
            link(nc.vector.tensor_tensor(stat[:, LO, :, :], stat32[:], stat[:, HI, :, :].bitcast(F32), ALU.subtract))

            def over(tab, n, rows=slice(0, P)):
                t = tab[rows, :]
                return t.unsqueeze(1).broadcast_to([t.shape[0], n, B])

            dve.wait_ge(l_edge, 32)
            for side in range(EDGES):
                p0 = 1 - side
                ins = nc.vector.tensor_tensor(xs_edge[:, side, p0:p0 + 6, :], x_edge[:, side, :, :].rearrange("p b t -> p t b"),
                                              over(s0, 6, slice(0, C)), ALU.mult)
            ins.then_inc(xs_edge_ready, 1)
            for side in range(EDGES):
                dve.wait_ge(he_psum, side + 1)
                link(nc.vector.tensor_tensor(h_raw[:, side, :, :], (tB, hB)[side][:, 0:5 * B].rearrange("p (t b) -> p t b", b=B),
                                             over(b0d, 5), ALU.add))
                p0 = 1 - side
                nc.vector.tensor_tensor(h_edge_s[:, side, p0:p0 + 5, :], h_raw[0:C, side, :, :],
                                        over(E1, 5, slice(0, C)), ALU.mult).then_inc(he_ready, 1)
            for r, n, h in ((slice(0, C), 1, h_raw[0:C, 1, 4, :]), (slice(C, P), 0, h_raw[C:P, 0, 0, :])):
                link(nc.vector.tensor_copy(h_col[r, HI, n, :], h))
                nc.vector.tensor_tensor(h_col[r, LO, n, :], h, h_col[r, HI, n, :].bitcast(F32), ALU.subtract)
            for side in range(EDGES):
                dve.wait_ge(ue_psum, side + 1)
                p0 = 1 - side
                u = u_edge[:, side, p0:p0 + 4, :]
                link(nc.vector.tensor_tensor(u, (rB, yB)[side][:, 0:4 * B].rearrange("p (t b) -> p t b", b=B), over(E2, 4), ALU.mult))
                link(nc.vector.tensor_tensor(u, u, over(u_bias, 4), ALU.add))
            nc.vector.tensor_tensor(u_edge[0:C, 0, 1, :], u_edge[0:C, 0, 1, :], u_bias8[0:C, :], ALU.subtract)
            nc.vector.tensor_tensor(u_edge[C:P, 1, 3, :], u_edge[C:P, 1, 3, :], u_bias8[C:P, :], ALU.subtract).then_inc(ue_ready, 1)
            dve.wait_ge(ve_psum, 1)
            for side in range(EDGES):
                p0 = 1 - side
                v = v_edge[:, side, p0:p0 + 3, :]
                link(nc.vector.tensor_tensor(v, qB[:, 3 * B * side:3 * B * side + 3 * B].rearrange("p (t b) -> p t b", b=B),
                                             over(E3, 3), ALU.mult))
                nc.vector.tensor_tensor(v, v, over(v_bias, 3), ALU.add)
            link(nc.vector.tensor_tensor(v_int[:], qB[:, 6 * B:7 * B], E3[:], ALU.mult))
            nc.vector.tensor_tensor(v_int[:], v_int[:], v_bias[:], ALU.add).then_inc(ve_ready, 1)
            dve.wait_ge(ye_psum, 1)
            d3 = d_all[:, 3, :].unsqueeze(1).broadcast_to([P, 3, B])
            link(nc.vector.tensor_tensor(y_fix[:], hB[:, 0:3 * B].rearrange("p (t b) -> p t b", b=B), d3, ALU.mult))
            nc.vector.tensor_scalar(y_fix[:], y_fix[:], smallT[:, L + 3:L + 4], None, ALU.add).then_inc(edges_ready, 1)

            def split_x(i, a, par):
                dve.wait_ge(xs_hi, upto(i, a))
                nc.vector.scalar_tensor_tensor(XS[:, a, LO, 0:S + 1], X[:, par, a, 0:T + 1:2], col(s0, i, a),
                                               XS[:, a, HI, 0:S + 1].bitcast(F32), ALU.mult, ALU.subtract).then_inc(xs_lo, 1)

            def scale_t(i, a):
                dve.wait_ge(t_hi, upto(i, a))
                nc.vector.scalar_tensor_tensor(TT[:, a, LO, :], t_const[:, :, :].rearrange("p w o -> p (w o)"), col(E3, i, a),
                                               TT[:, a, HI, :].bitcast(F32), ALU.mult, ALU.subtract).then_inc(t_lo, 1)

            def conv_out(i, a):
                dve.wait_ge(h_hi, upto(i, a))
                nc.vector.scalar_tensor_tensor(H[:, a, LO, 2:S + 1], hB[:, 1:S], col(b0d, i, a),
                                               H[:, a, HI, 2:S + 1].bitcast(F32), ALU.add, ALU.subtract).then_inc(h_lo, 1)
                dve.wait_ge(q_hi, upto(i, a))
                nc.vector.scalar_tensor_tensor(Q[:, a, LO, :], qB[:, 0:5 * C], col(E2, i, a),
                                               Q[:, a, HI, :].bitcast(F32), ALU.mult, ALU.subtract).then_inc(q_lo, 1)

            def r_out(i, a):
                dve.wait_ge(r_hi, upto(i, a))
                nc.vector.scalar_tensor_tensor(RR[0:C, a, LO, 0:7 * C], rB[0:C, 0:7 * C], E1[0:C, bass.ds(i * 2 + a, 1)],
                                               RR[0:C, a, HI, 0:7 * C].bitcast(F32), ALU.mult, ALU.subtract)
                nc.vector.scalar_tensor_tensor(RR[C:P, a, LO, C:8 * C], rB[C:P, 0:7 * C], E1[C:P, bass.ds(i * 2 + a, 1)],
                                               RR[C:P, a, HI, C:8 * C].bitcast(F32), ALU.mult, ALU.subtract).then_inc(r_lo, 1)

            def yt_out(i, a, par):
                dve.wait_ge(yt_hi, upto(i, a))
                nc.vector.tensor_tensor(YT[:, par, LO, :, C * a:C * a + C], tB[:, :].rearrange("p (c o) -> p c o", o=C),
                                        YT[:, par, HI, :, C * a:C * a + C].bitcast(F32), ALU.subtract).then_inc(yt_lo, 1)

            def route(j):
                zB = fB[0]
                dve.wait_ge(z_psum, j + 1)
                nc.vector.tensor_tensor(lg[:], zB[:, 0:E], ebias[:], ALU.add).then_inc(z_chain, 1)
                dve.wait_ge(z_chain, j * 6 + 1)
                nc.vector.tensor_reduce(lg_max[:], lg[:], AX_X, ALU.max).then_inc(z_chain, 1)
                dve.wait_ge(z_chain, j * 6 + 2)
                nc.vector.scalar_tensor_tensor(sc[:], lg[:], lg_max[:, 0:1], first_w[:], ALU.is_ge, ALU.mult).then_inc(z_chain, 1)
                dve.wait_ge(z_chain, j * 6 + 3)
                nc.vector.tensor_reduce(sc_max[:], sc[:], AX_X, ALU.max).then_inc(z_chain, 1)
                dve.wait_ge(z_chain, j * 6 + 4)
                nc.vector.scalar_tensor_tensor(zm[:, :].rearrange("p (e r) -> p e r", r=R),
                                               sc[:, :].unsqueeze(2).broadcast_to([P, E, R]), sc_max[:, 0:1],
                                               zB[:, E:GA].rearrange("p (e r) -> p e r", r=R),
                                               ALU.is_equal, ALU.mult).then_inc(z_chain, 1)
                dve.wait_ge(z_chain, j * 6 + 5)
                nc.vector.tensor_copy(zm3[:, 0::2, :], zm[:, :].unsqueeze(1).broadcast_to([P, 2, ER])).then_inc(z_chain, 1)
                dve.wait_ge(z_chain, j * 6 + 6)
                nc.vector.tensor_tensor(zm3[:, 1, :], zm[:], zm3[:, 0, :].bitcast(F32), ALU.subtract).then_inc(zm_ready, 1)

            def add(j, r, par, k, first=False):
                dve.wait_ge(f_psum, j * 3 + (r + 1))
                if r == 0:
                    dve.wait_ge(xr_landed[par], k * 16 + 16)
                    if not first:
                        dve.wait_ge(out_stored[par], k * 16)
                n0, n = REG[r]
                lo = max(n0, GA)
                nc.vector.tensor_tensor(OUT[:, par, lo - GA:n0 + n - GA], fB[r][:, lo - n0:n],
                                        XR[:, par, lo - GA:n0 + n - GA], ALU.add).then_inc(added, 1)

            def step(i, par, k, conv=True, ffn=True, ahead=True, first=False):
                kf = k - 1 + par
                if ffn:
                    yt_out(i - 1, 1, 1 - par)
                if conv:
                    conv_out(i, 0)
                    if ahead:
                        split_x(i + 1, 0, 1 - par)
                        scale_t(i + 1, 0)
                    r_out(i, 0)
                if ffn:
                    route(i - 1)
                if conv:
                    conv_out(i, 1)
                    if ahead:
                        split_x(i + 1, 1, 1 - par)
                        scale_t(i + 1, 1)
                    r_out(i, 1)
                if ffn:
                    for r in range(2):
                        add(i - 1, r, 1 - par, kf, first=isinstance(i, int) and i <= 2)
                if conv:
                    yt_out(i, 0, par)
                if ffn:
                    add(i - 1, 2, 1 - par, kf)

            for a in range(2):
                split_x(0, a, 0)
                scale_t(0, a)
            step(0, 0, 0, ffn=False, first=True)
            for n in range(N_WT):
                if n == 1:
                    dve.wait_ge(l_lb, 64)
                    lb = lb_nat[:, :, :, :].rearrange("p g e r -> p g (e r)")
                    nc.vector.tensor_copy(lb3[:, :, 0, :], lb)
                    link(nc.vector.tensor_copy(lb3[:, :, 1, :], lb))
                    nc.vector.tensor_tensor(lb3[:, :, 2, :], lb, lb3[:, :, 0, :].bitcast(F32), ALU.subtract).then_inc(lb3_ready, 1)
                if n > 2 * HB:
                    continue
                dve.wait_ge(wt_hi, n + 1)
                if n < 2 * HB:
                    c0, ob = CH // 2 * (n % 2), n // 2
                    w = slice(c0, c0 + CH // 2), slice(GA + P * ob, GA + P * ob + P)
                    src = fB[n % 3][:, :].rearrange("p (c o) -> p c o", o=P)
                else:
                    w = slice(0, CH), slice(0, GA)
                    src = fB[n % 3][:, 0:CH * GA].rearrange("p (c o) -> p c o", o=GA)
                nc.vector.tensor_tensor(WT[:, LO, w[0], w[1]], src, WT[:, HI, w[0], w[1]].bitcast(F32),
                                        ALU.subtract).then_inc(wt_lo, 1)
            dve.wait_ge(l_ga, 48)
            step(1, 1, 0)
            step(2, 0, 1)
            with dve.Fori(0, (PAIRS - 4) // 2) as k:
                step(k * 2 + 3, 1, k + 1)
                step(k * 2 + 4, 0, k + 2)
            step(PAIRS - 1, 1, PAIRS // 2 - 1, ahead=False)
            step(PAIRS, 0, PAIRS // 2, conv=False)

        @block.tensor
        def _(pe):
            pe.wait_ge(ident_ready, 1)
            pe.wait_ge(l_mod, 96)
            pe.transpose(qB[:, 0:B], cond_nat[:], ident[0:C, 0:C])
            pe.transpose(qB[:, B:B + 2 * L], small[:], ident[0:2 * L, 0:2 * L])
            for g in range(2):
                mm = pe.transpose(qB[:, P + P * g:2 * P + P * g], modw_nat[:, g, :], ident[:])
            mm.then_inc(modT_psum, 1)
            pe.wait_ge(w2_ready, 1)
            for i in range(L):
                mm = pe.transpose(hB[0:C, P * i:P * i + P], w2_sum[:, i, :], ident[:])
            mm.then_inc(w2T_psum, 1)
            pe.wait_ge(wdup_ready, 1)
            for n in range(3):
                for t in range(4):
                    mm = pe.transpose(fB[n][:, P * t:P * t + P],
                                      w_dup[:, 4 * n + t, :, :].rearrange("p a c -> p (a c)"), ident[:])
                mm.then_inc(wT_psum, 1)
            pe.wait_ge(modT_ready, 1)
            for i in range(L):
                mm = pe.matmul(rB[:, B * i:B * i + B], modwT[:, i, :, :].rearrange("p a c -> p (a c)"), condT[:],
                               start=True, stop=True)
            mm.then_inc(s_psum, 1)
            pe.wait_ge(s_ready, 1)
            pe.wait_ge(w2T_ready, 1)
            for i in range(L):
                mm = pe.matmul(yB[:, B * i:B * i + B], w2_sumT[:, i, :], s_sq[0:C, i, :], start=True, stop=True)
            mm.then_inc(d_psum, 1)
            pe.wait_ge(xs_edge_ready, 1)
            for side in range(EDGES):
                for k in range(K):
                    mm = pe.matmul((tB, hB)[side][:, 0:5 * B], wT[0:C, k, :], xs_edge[:, side, k:k + 5, :],
                                   start=(k == 0), stop=(k == K - 1))
                mm.then_inc(he_psum, 1)
            for side in range(EDGES):
                pe.wait_ge(he_ready, side + 1)
                for k in range(3):
                    mm = pe.matmul((rB, yB)[side][:, 0:4 * B], V1n[:, 2 * k:2 * k + 2, :].rearrange("p a c -> p (a c)"),
                                   h_edge_s[:, side, 2 - k:6 - k, :], start=(k == 0), stop=(k == 2))
                mm.then_inc(ue_psum, 1)
            pe.wait_ge(etab_ready, 1)
            pe.wait_ge(ue_ready, 1)
            for n, at in enumerate((1, 0, 2)):
                for side in range(EDGES):
                    pe.matmul(qB[:, 3 * B * side:3 * B * side + 3 * B], v_tab[:, n, :], u_edge[:, side, at:at + 3, :],
                              start=(n == 0 and side == 0), stop=(n == 2), skip_group_check=True)
                mm = pe.matmul(qB[:, 6 * B:7 * B], v_tab[:, n, :], u_bias[:], start=False, stop=(n == 2),
                               skip_group_check=True)
            mm.then_inc(ve_psum, 1)
            pe.wait_ge(ve_ready, 1)
            for j in range(4):
                pe.matmul(hB[:, 0:2 * B], y_tab[:, j, :], v_edge[:, :, j, :], start=(j == 0), stop=(j == 3),
                          skip_group_check=True)
                mm = pe.matmul(hB[:, 2 * B:3 * B], y_tab[:, j, :], v_int[:], start=False, stop=(j == 3),
                               skip_group_check=True)
            mm.then_inc(ye_psum, 1)

            PASS = ((HI, HI), (HI, LO), (LO, HI))

            def conv_h(i, a, first=False):
                pe.wait_ge(xs_lo, upto(i, a))
                if not first or a:
                    pe.wait_ge(h_lo, upto(i, a) - 1)
                for n, (w, m) in enumerate(PASS):
                    for t in range(2):
                        mm = pe.matmul(hB[:, :], stat[:, w, t, :], XS[:, a, m, t:t + S],
                                       start=(n == 0 and t == 0), stop=(n == 2 and t == 1))
                mm.then_inc(h_psum, 1)

            def make_q(i, a, first=False):
                pe.wait_ge(t_lo, upto(i, a))
                if not first or a:
                    pe.wait_ge(q_lo, upto(i, a) - 1)
                for n, (w, m) in enumerate(PASS):
                    for t in range(2):
                        mm = pe.matmul(qB[:, C * t:C * t + 4 * C], stat[:, w, 2 + t, :], TT[:, a, m, :],
                                       start=(n == 0 and t == 0), stop=(n == 2), skip_group_check=True)
                mm.then_inc(q_psum, 1)

            def make_r(i, a, first=False):
                pe.wait_ge(q_lo, upto(i, a))
                if not first or a:
                    pe.wait_ge(r_lo, upto(i, a) - 1)
                for n, (w, m) in enumerate(PASS):
                    for t in range(3):
                        mm = pe.matmul(rB[:, C * t:C * t + 5 * C], stat[:, w, 4 + t, :], Q[:, a, m, :],
                                       start=(n == 0 and t == 0), stop=(n == 2), skip_group_check=True)
                mm.then_inc(r_psum, 1)

            def conv_y(i, a, first=False):
                pe.wait_ge(r_lo, upto(i, a))
                pe.wait_ge(h_lo, upto(i, a))
                pe.wait_ge(h_cols, upto(i, a))
                if not first or a:
                    pe.wait_ge(y_mid, upto(i, a) - 1)
                for n, (w, m) in enumerate(PASS):
                    for t in range(4):
                        r0 = C * (6 - 2 * t)
                        mm = pe.matmul(yB[:, :], RR[:, a, w, r0:r0 + P], H[:, a, m, t:t + S],
                                       start=(n == 0 and t == 0), stop=(n == 2 and t == 3))
                mm.then_inc(y_psum, 1)

            def turn_y(i, a, first=False, z=True):
                pe.wait_ge(y_mid, upto(i, a))
                pe.wait_ge(y_cols, upto(i, a))
                if not first or a:
                    pe.wait_ge(yt_lo, upto(i, a) - 1)
                if z:
                    pe.wait_ge(zt_ready, i)
                for s in range(SB):
                    mm = pe.transpose(tB[:, P * s:P * s + P], Y[:, a, P * s:P * s + P], ident[:])
                mm.then_inc(yt_psum, 1)

            def ffn(j, r, par, chunks, first=False):
                if chunks[0] == 0:
                    if not first:
                        pe.wait_ge(added, j * 3 - (2 - r))
                    pe.wait_ge(yt_lo, upto(j, 1))
                n0, n = REG[r]
                for c in chunks:
                    for q, (w, m) in enumerate(PASS):
                        mm = pe.matmul(fB[r][:, 0:n], YT[:, par, w, c, :], WT[:, m, c, n0:n0 + n],
                                       start=(c == 0 and q == 0), stop=(c == CH - 1 and q == 2))
                return mm

            def turn_z(j):
                pe.wait_ge(zm_ready, j + 1)
                pe.wait_ge(yt_lo, upto(j, 1))
                pe.transpose(tB[0:3 * ER, 0:P], zm3[:, :, :].rearrange("p a z -> p (a z)").bitcast(F32),
                             ident[:]).then_inc(zt_psum, 1)

            def low_rank(j, r):
                n0, n = REG[r]
                lo = max(n0, GA)
                pe.matmul(fB[r][:, lo - n0:n], zT[:], BT[:, lo - GA:n0 + n - GA], start=False, stop=True,
                          skip_group_check=True).then_inc(f_psum, 1)

            def step(i, par, conv=True, do_ffn=True, first=False):
                ffn_first = isinstance(i, int) and i == 1
                j, q = i - 1, 1 - par
                if conv:
                    conv_h(i, 0, first)
                    make_q(i, 0, first)
                if do_ffn:
                    ffn(j, 0, q, range(CH), ffn_first).then_inc(z_psum, 1)
                if conv:
                    make_r(i, 0, first)
                    conv_h(i, 1, first)
                    make_q(i, 1, first)
                if do_ffn:
                    ffn(j, 1, q, range(CH), ffn_first)
                if conv:
                    make_r(i, 1, first)
                    conv_y(i, 0, first)
                if do_ffn:
                    turn_z(j)
                    ffn(j, 2, q, range(CH // 2), ffn_first)
                    pe.wait_ge(zt_ready, i)
                    low_rank(j, 0)
                    low_rank(j, 1)
                if conv:
                    turn_y(i, 0, first, z=do_ffn)
                    conv_y(i, 1, first)
                if do_ffn:
                    ffn(j, 2, q, range(CH // 2, CH), ffn_first)
                    low_rank(j, 2)
                if conv:
                    turn_y(i, 1, first, z=False)

            step(0, 0, do_ffn=False, first=True)
            for n in range(N_WT):
                if n >= 3:
                    pe.wait_ge(wt_lo, n - 2)
                if n < 2 * HB:
                    ob = n // 2
                    if n % 2 == 0:
                        pe.wait_ge(l_wup[ob % 4], 16 * (ob // 4 + 1))
                    for t in range(CH // 2):
                        c = CH // 2 * (n % 2) + t
                        t0 = 2 * P * (c // 2) + c % 2
                        mm = pe.transpose(fB[n % 3][:, P * t:P * t + P],
                                          wup_nat[:, ob % 4, t0:t0 + 2 * P - 1:2], ident[:])
                elif n == 2 * HB:
                    pe.wait_ge(l_ga, 48)
                    for c in range(CH):
                        t0 = 2 * P * (c // 2) + c % 2
                        mm = pe.transpose(fB[n % 3][:, GA * c:GA * c + GA], ga_nat[:, t0:t0 + 2 * P - 1:2],
                                          ident[0:GA, 0:GA])
                else:
                    pe.wait_ge(lb3_ready, 1)
                    for t in range(4):
                        g = 4 * (n - 2 * HB - 1) + t
                        mm = pe.transpose(fB[n % 3][0:3 * ER, P * t:P * t + P],
                                          lb3[:, g, :, :].rearrange("p a z -> p (a z)").bitcast(F32), ident[:])
                mm.then_inc(wt_psum, 1)
            pe.wait_ge(wt_hi, N_WT)
            pe.wait_ge(wt_lo, 2 * HB + 1)
            step(1, 1)
            with pe.Fori(0, (PAIRS - 2) // 2) as k:
                step(k * 2 + 2, 0)
                step(k * 2 + 3, 1)
            step(PAIRS, 0, conv=False)


_INS = ["x", "cond_512", "L0_cond_weights", "L0_cond_biases", "L0_cond_mod_w", "L0_cond_mod_b", "L0_ffn_W_up",
        "L0_ffn_gate_w", "L0_ffn_expert_bias", "L0_ffn_lora_A", "L0_ffn_lora_B"]


def kernel(**inputs):
    import numpy as _np
    import concourse.bacc as _bacc
    from concourse import mybir as _mybir
    from concourse.bass_utils import run_bass_kernel_spmd as _run

    nc = _bacc.Bacc("TRN2", target_bir_lowering=False, num_devices=1)
    arrays, args = {}, []
    for name in _INS:
        a = _np.ascontiguousarray(inputs[name])
        arrays[f"in_{name}_dram"] = a
        args.append(nc.dram_tensor(f"in_{name}_dram", a.shape, _mybir.dt.from_np(a.dtype), kind="ExternalInput").ap())
    out = nc.dram_tensor("out_dram", inputs["x"].shape, _mybir.dt.float32, kind="ExternalOutput").ap()
    adaln_ffn_kernel(nc, *args, out)
    r = _run(nc, [arrays], core_ids=[0])
    return r.results[0]["out_dram"]
```

```python
from contextlib import ExitStack

import concourse.bass as bass
from concourse import mybir

F32 = mybir.dt.float32
F32R = mybir.dt.float32r
ALU = mybir.AluOpType
ACT = mybir.ActivationFunctionType
AX_X = mybir.AxisListType.X

P = 128
HI, LO = 0, 1


def adaln_ffn_kernel(
    nc: bass.Bass,
    x: bass.AP,
    cond: bass.AP,
    conv_w: bass.AP,
    conv_b: bass.AP,
    mod_w: bass.AP,
    mod_b: bass.AP,
    W_up: bass.AP,
    gate_w: bass.AP,
    expert_bias: bass.AP,
    lora_A: bass.AP,
    lora_B: bass.AP,
    out: bass.AP,
):
    B, C, T = x.shape
    L, _, _, K = conv_w.shape
    D = cond.shape[1]
    E = gate_w.shape[0]
    R = lora_A.shape[1]
    ER = E * R
    PAIRS = B // 2
    S = T // 2
    SB = S // P
    CH = 2 * SB
    GA = E + ER
    NW = GA + T
    SCALE = float(1.0 / (C * K) ** 0.5)
    EPS = 1e-8
    BLUR = [0.125, 0.375, 0.375, 0.125]
    M = 6
    HB = T // P
    REG = [(0, 354), (354, 354), (708, 352)]
    assert C == 64 and P == 2 * C and T == 1024 and D == P and L == 4 and K == 3 and NW == 1060
    EDGES = 2

    ctx = ExitStack()
    with ctx:
        def sb(name, shape, dt=F32):
            return ctx.enter_context(nc.sbuf_tensor(name, shape, dt))

        def pb(name):
            return ctx.enter_context(nc.psum_tensor(name, [P, 512], F32))

        def sem(name):
            return ctx.enter_context(nc.semaphore(name))

        ga_nat = sb("ga_nat", [GA, T])
        lb_nat = sb("lb_nat", [P, HB, E, R])
        ebias = sb("ebias", [P, E])
        ident = sb("ident", [P, P])
        smallT = sb("smallT", [P, 2 * L])
        d_all = sb("d_all", [P, L, B])
        s0 = sb("s0", [P, B])
        E1 = sb("E1", [P, B])
        E2 = sb("E2", [P, B])
        E3 = sb("E3", [P, B])
        b0d = sb("b0d", [P, B])
        h_col = sb("h_col", [P, 2, B])
        y_fix = sb("y_fix", [P, 3, B])
        stat = sb("stat", [P, 2, 8, P], F32R)
        t_const = sb("t_const", [P, 4, C])
        condT = sb("condT", [D, B])
        s_all = sb("s_all", [P, L, B])
        var = sb("var", [P, L, B])
        rt_tmp = sb("rt_tmp", [P, L, B])
        wT = sb("wT", [P, L * K, P])
        V1T = sb("V1T", [P, M, C])
        V3T = sb("V3T", [P, M, C])
        stat32 = sb("stat32", [P, 8, P])
        V1n = sb("V1n", [C, M, C])
        v_int = sb("v_int", [P, B])
        w_sq = wT[:, 0:L * C * K // P, :]
        s2 = sb("s2", [P, B])
        s3 = sb("s3", [P, B])
        u_bias = sb("u_bias", [P, B])
        u_bias8 = sb("u_bias8", [P, B])
        v_bias = sb("v_bias", [P, B])
        WT = sb("WT", [P, 2, CH, NW], F32R)
        with ExitStack() as early:
            w_nat = early.enter_context(nc.sbuf_tensor("w_nat", [P, L, C * K], F32))
            modw_nat = early.enter_context(nc.sbuf_tensor("modw_nat", [P, 2, D], F32))
            modwT = early.enter_context(nc.sbuf_tensor("modwT", [D, L, 2, C], F32))
            s_sq = early.enter_context(nc.sbuf_tensor("s_sq", [P, L, B], F32))
        BT = sb("BT", [3 * ER, T], F32R)
        lb3 = sb("lb3", [P, HB, 3, ER], F32R)
        first_w = sb("first_w", [P, E])
        X = sb("X", [P, 2, T + 2])
        XS = sb("XS", [P, 2, 2, 3, S // 2], F32R)
        H = sb("H", [P, 2, 2 * (S + 4)])
        G = sb("G", [P, 2, 2, 3, S // 2 + 2], F32R)
        TT = sb("TT", [P, 2, 2, 4 * C], F32R)
        Q = sb("Q", [P, 2, 5 * C], F32R)
        R32 = sb("R32", [P, 12 * C])
        with ExitStack() as early:
            w2_sum = early.enter_context(nc.sbuf_tensor("w2_sum", [P, L, C], F32))
            w2_sumT = early.enter_context(nc.sbuf_tensor("w2_sumT", [C, L, P], F32))
            w_dup = early.enter_context(nc.sbuf_tensor("w_dup", [P, L * K, 2, C], F32))
            cond_nat = early.enter_context(nc.sbuf_tensor("cond_nat", [C, D], F32))
            small = early.enter_context(nc.sbuf_tensor("small", [2 * L, P], F32))
        RR = sb("RR", [P, 2, 2, 12 * C], F32R)
        mid = sb("mid", [P, S])
        with ExitStack() as edge:
            def tmp(name, shape, dt=F32):
                return edge.enter_context(nc.sbuf_tensor(name, shape, dt))

            x_edge = tmp("x_edge", [C, EDGES, B, 6])
            v_tab = tmp("v_tab", [P, 3, P])
            y_tab = tmp("y_tab", [P, 4, P])
            xs_edge = tmp("xs_edge", [C, EDGES, 7, B])
            h_raw = tmp("h_raw", [P, EDGES, 5, B])
            h_edge_s = tmp("h_edge_s", [C, EDGES, 6, B])
            u_edge = tmp("u_edge", [P, EDGES, 5, B])
            v_edge = tmp("v_edge", [P, EDGES, 4, B])
        Y = sb("Y", [P, 2, S])
        YT = sb("YT", [P, 2, 2, CH, P], F32R)
        rows = sb("rows", [P, 3, T])
        OUT, XR = rows[:, 0:2, :], rows[:, 2, :]
        wup_nat = rows
        lg = sb("lg", [P, E])
        lg_max = sb("lg_max", [P, 1])
        sc = sb("sc", [P, E])
        sc_max = sb("sc_max", [P, 1])
        zm = sb("zm", [P, ER])
        zm3 = sb("zm3", [P, 3, ER], F32R)
        zT = sb("zT", [3 * ER, P], F32R)

        hrB = ctx.enter_context(nc.psum_tensor("hrB", [P, 2, 512], F32))
        hB, rB = hrB[:, 0, :], hrB[:, 1, :]
        qB, yB, tB = pb("qB"), pb("yB"), pb("tB")
        fB = [pb("zB"), pb("f1B"), pb("f2B")]

        l_mod = sem("l_mod")
        l_w = sem("l_w")
        l_bias = sem("l_bias")
        l_edge = sem("l_edge")
        l_wup = [sem(f"l_wup{n}") for n in range(3)]
        l_ga = sem("l_ga")
        l_lb = sem("l_lb")
        ident_ready = sem("ident_ready")
        pool_zero = sem("pool_zero")
        dve_setup = sem("dve_setup")
        modT_psum = sem("modT_psum")
        modT_ready = sem("modT_ready")
        s_psum = sem("s_psum")
        s_ready = sem("s_ready")
        w2_ready = sem("w2_ready")
        w2T_psum = sem("w2T_psum")
        w2T_ready = sem("w2T_ready")
        w_dup_ready = sem("w_dup_ready")
        wT_psum = sem("wT_psum")
        wT_ready = sem("wT_ready")
        d_psum = sem("d_psum")
        var_ready = sem("var_ready")
        root_ready = sem("root_ready")
        l0_tables = sem("l0_tables")
        l0_sum = sem("l0_sum")
        s0_ready = sem("s0_ready")
        scales_ready = sem("scales_ready")
        v1_ready = sem("v1_ready")
        v3_ready = sem("v3_ready")
        act_tables = sem("act_tables")
        stat_hi = sem("stat_hi")
        stat_lo = sem("stat_lo")
        xs_edge_ready = sem("xs_edge_ready")
        he_psum = sem("he_psum")
        he_ready = sem("he_ready")
        h_col_ready = sem("h_col_ready")
        ue_psum = sem("ue_psum")
        ue_ready = sem("ue_ready")
        ve_psum = sem("ve_psum")
        ve_ready = sem("ve_ready")
        ye_psum = sem("ye_psum")
        edges_ready = sem("edges_ready")
        etab_ready = sem("etab_ready")
        lb3_ready = sem("lb3_ready")
        wt_psum = sem("wt_psum")
        wt_hi = sem("wt_hi")
        wt_lo = sem("wt_lo")
        x_landed = sem("x_landed")
        xr_landed = sem("xr_landed")
        out_stored = [sem(f"out_stored{p}") for p in range(2)]
        x_diff, h_psum, h_mid = sem("x_diff"), sem("h_psum"), sem("h_mid")
        xs_hi, xs_lo = sem("xs_hi"), sem("xs_lo")
        t_hi, t_lo = sem("t_hi"), sem("t_lo")
        h_out, h_cols, h_diff = sem("h_out"), sem("h_cols"), sem("h_diff")
        h_hi, h_lo = sem("h_hi"), sem("h_lo")
        q_psum, q_hi, q_lo = sem("q_psum"), sem("q_hi"), sem("q_lo")
        r_psum, r_lower, r_upper, r_sum = sem("r_psum"), sem("r_lower"), sem("r_upper"), sem("r_sum")
        r_hi, r_lo = sem("r_hi"), sem("r_lo")
        y_psum, y_x2, y_out, y_cols = sem("y_psum"), sem("y_x2"), sem("y_out"), sem("y_cols")
        yt_psum, yt_hi, yt_lo = sem("yt_psum"), sem("yt_hi"), sem("yt_lo")
        z_psum = sem("z_psum")
        z_chain = sem("z_chain")
        zm_ready = sem("zm_ready")
        zt_psum = sem("zt_psum")
        zt_ready = sem("zt_ready")
        f_psum = sem("f_psum")
        added = sem("added")

        LATE = 4
        NW_EARLY = 2 * HB - LATE
        NB = NW_EARLY + 3

        def upto(i, a):
            return i * 2 + (a + 1)

        def w_up_place(part, h):
            c0, o0 = CH // 2 * (h % 2), GA + P * (h // 2)
            return WT[:, part, c0:c0 + CH // 2, o0:o0 + P]

        def col(tab, i, a):
            return tab[:, bass.ds(i * 2 + a, 1)]

        x_conv = x.rearrange("(i a) c t -> i c a t", a=2)
        x_rows = x.rearrange("(i a) c t -> i (a c) t", a=2)
        out_rows = out.rearrange("(i a) c t -> i (a c) t", a=2)

        block = ctx.enter_context(nc.Block())

        @block.sync
        def _(sp):
            sp.dma_start(cond_nat[:], cond).then_inc(l_mod, 16)
            sp.dma_start(modw_nat[:], mod_w.rearrange("i c d -> (i c) d").rearrange("(g p) d -> p g d", p=P)).then_inc(l_mod, 16)
            for half in range(2):
                sp.dma_start(w_nat[C * half:C * half + C, :, :],
                             conv_w.rearrange("i o c k -> o i (c k)")).then_inc(l_w, 16)
            for n, rows in enumerate((mod_b, conv_b)):
                for half in range(2):
                    sp.dma_start(small[L * n:L * n + L, C * half:C * half + C], rows).then_inc(l_bias, 16)

            def load_x(i):
                sp.dma_start(X[0:C, :, 2:T + 2], x_conv[i]).then_inc(x_landed, 16)
                sp.dma_start(X[C:P, :, 1:T + 1], x_conv[i]).then_inc(x_landed, 16)

            load_x(0)
            sp.dma_start(wup_nat[:, 0, :], W_up[0:P, :]).then_inc(l_wup[0], 16)
            sp.dma_start(x_edge[:, 0, :, :], x[:, :, 0:6].rearrange("b c t -> c b t")).then_inc(l_edge, 16)
            sp.dma_start(x_edge[:, 1, :, :], x[:, :, T - 6:T].rearrange("b c t -> c b t")).then_inc(l_edge, 16)
            for n in range(1, 3):
                sp.dma_start(wup_nat[:, n, :], W_up[P * n:P * n + P, :]).then_inc(l_wup[n], 16)
            sp.dma_start(ebias[:], expert_bias.partition_broadcast(P)).then_inc(l_ga, 16)
            sp.dma_start(ga_nat[0:E, :], gate_w).then_inc(l_ga, 16)
            sp.dma_start(ga_nat[E:GA, :], lora_A.rearrange("e r h -> (e r) h")).then_inc(l_ga, 16)
            for e in range(E):
                sp.dma_start(lb_nat[:, :, e, :], lora_B[e].rearrange("(g p) r -> p g r", p=P)).then_inc(l_lb, 16)
            for n in range(3, HB):
                sp.wait_ge(wt_psum, 2 * (n - 2))
                sp.dma_start(wup_nat[:, n % 3, :], W_up[P * n:P * n + P, :]).then_inc(l_wup[n % 3], 16)
                if n == 3:
                    sp.wait_ge(xs_lo, 2)
                    load_x(1)

            def step(i, par, load=True, xr=True, store=True):
                if load:
                    sp.wait_ge(xs_lo, upto(i + 1, 1))
                    load_x(i + 2)
                if store:
                    sp.wait_ge(added, i * 3)
                    sp.dma_start(out_rows[i - 1], OUT[:, 1 - par, :]).then_inc(out_stored[1 - par], 16)
                if xr:
                    sp.dma_start(XR, x_rows[i]).then_inc(xr_landed, 16)

            sp.wait_ge(wt_psum, NW_EARLY)
            step(0, 0, store=False)
            step(1, 1)
            with sp.Fori(0, (PAIRS - 4) // 2) as k:
                step(k * 2 + 2, 0)
                step(k * 2 + 3, 1)
            step(PAIRS - 2, 0, load=False)
            step(PAIRS - 1, 1, load=False)
            step(PAIRS, 0, load=False, xr=False)
            for par in range(2):
                sp.wait_ge(out_stored[par], 16 * (PAIRS // 2))

        @block.gpsimd
        def _(pool):
            nc.gpsimd.memset(ident[:], 0.0).then_inc(pool_zero, 1)
            pool.wait_ge(pool_zero, 1)
            nc.gpsimd.affine_select(out=ident[:], in_=ident[:], compare_op=ALU.not_equal, fill=1.0,
                                    base=0, pattern=[[-1, P]], channel_multiplier=1).then_inc(ident_ready, 1)
            nc.gpsimd.memset(V1n[:], 0.0)
            nc.gpsimd.memset(V1T[:], 0.0)
            nc.gpsimd.memset(V3T[:], 0.0)
            nc.gpsimd.memset(stat32[:], 0.0)
            nc.gpsimd.memset(t_const[:], 0.0).then_inc(pool_zero, 1)
            nc.gpsimd.memset(X[:, :, 0:1], 0.0)
            nc.gpsimd.memset(xs_edge[:], 0.0)
            nc.gpsimd.memset(h_edge_s[:], 0.0)
            nc.gpsimd.memset(u_edge[:], 0.0)
            nc.gpsimd.memset(v_edge[:], 0.0)
            nc.gpsimd.memset(v_tab[:], 0.0)
            nc.gpsimd.memset(y_tab[:], 0.0)
            nc.gpsimd.memset(h_col[:], 0.0)
            nc.gpsimd.memset(H[:, :, 0:1], 0.0)
            nc.gpsimd.memset(H[:, :, 2 * S + 4:2 * S + 8], 0.0)
            nc.gpsimd.memset(R32[:], 0.0)
            for e in range(E):
                ins = nc.gpsimd.memset(first_w[:, e:e + 1], float(E - e))
            ins.then_inc(pool_zero, 1)

            def x_differences(i):
                pool.wait_ge(x_landed, i * 32 + 32)
                for d in range(2):
                    ins = nc.gpsimd.tensor_tensor(X[:, :, 2 * d + 1:T:4], X[:, :, 4 * d:4 * d + T - 3:4], X[:, :, 2:T:4],
                                                  ALU.subtract)
                ins.then_inc(x_diff, 1)

            def h_columns(i, a):
                pool.wait_ge(h_out, upto(i, a))
                nc.gpsimd.tensor_copy(H[:, a, 2:2 * S + 3:2 * S].unsqueeze(2),
                                      h_col[:, :, bass.ds(i * 2 + a, 1)]).then_inc(h_cols, 1)

            def y_columns(i, a):
                pool.wait_ge(y_out, upto(i, a))
                nc.gpsimd.tensor_copy(Y[:, a, 0:S:S - 1].unsqueeze(2),
                                      y_fix[:, 0:2, bass.ds(i * 2 + a, 1)]).then_inc(y_cols, 1)

            def step(i, ahead=True):
                for a in range(2):
                    h_columns(i, a)
                if ahead:
                    x_differences(i + 1)
                for a in range(2):
                    y_columns(i, a)

            pool.wait_ge(pool_zero, 3)
            x_differences(0)
            pool.wait_ge(l0_tables, 1)
            nc.gpsimd.tensor_tensor(stat32[:, 7, :], stat32[:, 0, :], stat32[:, 1, :], ALU.add).then_inc(l0_sum, 1)
            pool.wait_ge(h_col_ready, 1)
            for a in range(2):
                h_columns(0, a)
            x_differences(1)
            pool.wait_ge(l_lb, 64)
            lb = lb_nat[:, :, :, :].rearrange("p g e r -> p g (e r)")
            nc.gpsimd.tensor_copy(lb3[:, :, 0, :], lb)
            nc.gpsimd.tensor_copy(lb3[:, :, 1, :], lb).then_inc(pool_zero, 1)
            pool.wait_ge(pool_zero, 4)
            nc.gpsimd.tensor_tensor(lb3[:, :, 2, :], lb, lb3[:, :, 0, :].bitcast(F32), ALU.subtract).then_inc(lb3_ready, 1)
            pool.wait_ge(edges_ready, 1)
            for a in range(2):
                y_columns(0, a)
            with pool.Fori(1, PAIRS - 1) as i:
                step(i)
            step(PAIRS - 1, ahead=False)

        @block.scalar
        def _(act):
            act.wait_ge(ident_ready, 1)
            nc.scalar.activation(mid[:, 0:1], ident[:, 0:1], ACT.Sqrt)
            wv = w_nat[:, :, :].rearrange("p i (c k) -> p i k c", k=K)
            act.wait_ge(l_w, 32)
            for i in range(L):
                ins = nc.scalar.activation(w_dup[:, K * i:K * i + K, :, :],
                                           wv[:, i, :, :].unsqueeze(2).broadcast_to([P, K, 2, C]), ACT.Copy)
            ins.then_inc(w_dup_ready, 1)
            act.wait_ge(w_dup_ready, 1)

            def taps(n):
                act.wait_ge(wT_psum, n + 1)
                if n == 0:
                    act.wait_ge(w2_ready, 1)
                nc.scalar.activation(wT[:, 4 * n:4 * n + 4, :], fB[n][:, :].rearrange("p (t o) -> p t o", o=P),
                                     ACT.Copy).then_inc(wT_ready, 1)

            T0, T2 = 0, 2 * K
            act.wait_ge(pool_zero, 2)
            for r0, c0, tab, tap in ((0, 0, 2, 2), (C, 0, 2, 1), (C, C, 2, 2), (0, 0, 3, 0), (0, C, 3, 1), (C, C, 3, 0)):
                nc.scalar.activation(stat32[r0:r0 + C, tab, c0:c0 + C], w_dup[r0:r0 + C, T2 + tap, 0, :], ACT.Copy)
            taps(0)
            taps(1)
            act.wait_ge(wT_ready, 1)
            for r0, c0, tab, tap in ((0, 0, 0, 0), (C, 0, 0, 1), (C, C, 0, 0), (0, 0, 1, 2), (0, C, 1, 1), (C, C, 1, 2)):
                ins = nc.scalar.activation(stat32[r0:r0 + C, tab, c0:c0 + C], wT[r0:r0 + C, T0 + tap, c0:c0 + C], ACT.Copy)
            ins.then_inc(l0_tables, 1)
            act.wait_ge(var_ready, 1)
            nc.scalar.activation(rt_tmp[:], var[:], ACT.Sqrt).then_inc(root_ready, 1)
            taps(2)
            act.wait_ge(v1_ready, 1)
            for e in range(2):
                r = slice(C * e, C * e + C)
                ins = nc.scalar.activation(stat32[r, 4:7, :].rearrange("p t (a c) -> p t a c", a=2),
                                           V1T[r, e::2, :].unsqueeze(2).broadcast_to([C, 3, 2, C]), ACT.Copy)
            ins.then_inc(act_tables, 1)
            act.wait_ge(act_tables, 1)
            act.wait_ge(l0_sum, 1)
            nc.scalar.activation(stat[:, HI, :, :], stat32[:], ACT.Copy).then_inc(stat_hi, 1)

            def t_tables():
                act.wait_ge(v3_ready, 1)
                for w in range(3):
                    nc.scalar.activation(t_const[0:C, w, :], V3T[0:C, 5 - 2 * w, :], ACT.Copy)
                    ins = nc.scalar.activation(t_const[C:P, w + 1, :], V3T[C:P, 4 - 2 * w, :], ACT.Copy)
                ins.then_inc(act_tables, 1)
                act.wait_ge(act_tables, 2)

            def edge_tables():
                act.wait_ge(pool_zero, 3)
                for r0, c0, tab, tap in ((0, 0, 0, 1), (0, C, 0, 0), (C, 0, 0, 2), (C, C, 0, 1), (C, 0, 1, 0), (0, C, 2, 2)):
                    nc.scalar.activation(v_tab[r0:r0 + C, tab, c0:c0 + C], wT[r0:r0 + C, T2 + tap, c0:c0 + C], ACT.Copy)
                for e in range(2):
                    r = slice(C * e, C * e + C)
                    nc.scalar.activation(y_tab[r, 0:3, 0:C], V3T[r, e::2, :], ACT.Copy)
                    tail = nc.scalar.activation(y_tab[r, 1:4, C:P], V3T[r, e::2, :], ACT.Copy)
                tail.then_inc(etab_ready, 1)

            def split_x(i, a, first=False):
                act.wait_ge(x_diff, i + 1)
                if not first:
                    act.wait_ge(h_psum, i)
                nc.scalar.activation(XS[:, a, HI, :, :], X[:, a, 1:T + 1].rearrange("p (m g) -> p g m", g=4)[:, 0:3, :],
                                     ACT.Copy, scale=col(s0, i, a)).then_inc(xs_hi, 1)

            def scale_t(i, a, first=False):
                if not first:
                    act.wait_ge(q_psum, upto(i, a) - 2)
                nc.scalar.activation(TT[:, a, HI, :], t_const[:], ACT.Copy, scale=col(E3, i, a)).then_inc(t_hi, 1)

            def h_from_psum(i):
                act.wait_ge(h_psum, i + 1)
                nc.scalar.activation(mid[:], yB[:], ACT.Copy).then_inc(h_mid, 1)

            def q_split(i, a):
                act.wait_ge(q_psum, upto(i, a))
                if not isinstance(i, int) or i or a:
                    act.wait_ge(r_psum, upto(i, a) - 1)
                nc.scalar.activation(Q[:, HI, :], qB[:, 0:5 * C], ACT.Copy, scale=col(E2, i, a)).then_inc(q_hi, 1)

            def h_split(i, a, first=False):
                act.wait_ge(h_diff, upto(i, a))
                if not first:
                    act.wait_ge(y_psum, upto(i, a) - 2)
                nc.scalar.activation(G[:, a, HI, :, 0:S // 2 + 1],
                                     H[:, a, 1:2 * S + 5].rearrange("p (m g) -> p g m", g=4)[:, 0:3, :],
                                     ACT.Copy).then_inc(h_hi, 1)

            def r_from_psum(i, a):
                act.wait_ge(r_psum, upto(i, a))
                if not isinstance(i, int) or i or a:
                    act.wait_ge(r_lo, upto(i, a) - 1)
                if not isinstance(i, int) or i or a:
                    act.wait_ge(r_lo, upto(i, a) - 1)
                nc.scalar.activation(R32[0:C, 0:7 * C], rB[0:C, 0:7 * C], ACT.Copy,
                                     scale=E1[0:C, bass.ds(i * 2 + a, 1)]).then_inc(r_lower, 1)

            def r_split(i, a, first=False):
                act.wait_ge(r_sum, upto(i, a))
                if not first:
                    act.wait_ge(y_psum, upto(i, a) - 2)
                nc.scalar.activation(RR[:, a, HI, :], R32[:], ACT.Copy).then_inc(r_hi, 1)

            def y_from_psum(i, a):
                act.wait_ge(y_psum, upto(i, a))
                if a:
                    act.wait_ge(y_out, upto(i, 0))
                nc.scalar.activation(mid[:, 0:S // 2], hB[:, 0:S // 2], ACT.Identity,
                                     scale=d_all[:, 3, bass.ds(i * 2 + a, 1)],
                                     bias=y_fix[:, 2, bass.ds(i * 2 + a, 1)]).then_inc(y_x2, 1)

            def yt_out(i, a, par, wait=True):
                act.wait_ge(yt_psum, upto(i, a))
                if wait:
                    act.wait_ge(f_psum, i * 3 - 3)
                nc.scalar.activation(YT[:, par, HI, :, C * a:C * a + C],
                                     tB[:, :].rearrange("p (c o) -> p c o", o=C), ACT.Copy).then_inc(yt_hi, 1)

            def step(i, par, conv=True, ffn=True, ahead=True, late=False):
                if conv:
                    q_split(i, 0)
                if ffn:
                    yt_out(i - 1, 1, 1 - par, wait=not (isinstance(i, int) and i <= 2))
                if conv:
                    h_from_psum(i)
                    if late:
                        late_bank(0)
                    h_split(i, 0)
                    if late:
                        late_bank(1)
                    r_from_psum(i, 0)
                    q_split(i, 1)
                    r_split(i, 0)
                    h_split(i, 1)
                    if ahead:
                        scale_t(i + 1, 0)
                    if late:
                        late_bank(2)
                    r_from_psum(i, 1)
                    r_split(i, 1)
                    if late:
                        late_bank(3)
                    y_from_psum(i, 0)
                if ffn:
                    act.wait_ge(zt_psum, i)
                    nc.scalar.activation(zT[:], tB[0:3 * ER, 0:P], ACT.Copy).then_inc(zt_ready, 1)
                if conv:
                    if ahead:
                        split_x(i + 1, 0)
                        split_x(i + 1, 1)
                    yt_out(i, 0, par, wait=not (isinstance(i, int) and i < 2))
                    y_from_psum(i, 1)
                    if ahead:
                        scale_t(i + 1, 1)

            def w_bank(n0, n1):
                for n in range(n0, n1):
                    act.wait_ge(wt_psum, n + 1)
                    if n < NW_EARLY:
                        dst, src = w_up_place(HI, n), fB[n % 3][:, :].rearrange("p (c o) -> p c o", o=P)
                    elif n == NW_EARLY:
                        dst, src = WT[:, HI, :, 0:GA], fB[n % 3][:, 0:CH * GA].rearrange("p (c o) -> p c o", o=GA)
                    else:
                        h0 = 512 * (n - NW_EARLY - 1)
                        dst, src = BT[:, h0:h0 + 512], fB[n % 3][0:3 * ER, :]
                    nc.scalar.activation(dst, src, ACT.Copy).then_inc(wt_hi, 1)

            def late_bank(m):
                act.wait_ge(wt_psum, NB + m + 1)
                nc.scalar.activation(w_up_place(HI, NW_EARLY + m), fB[2][:, :].rearrange("p (c o) -> p c o", o=P),
                                     ACT.Copy).then_inc(wt_hi, 1)

            act.wait_ge(pool_zero, 3)
            act.wait_ge(s0_ready, 1)
            split_x(0, 0, first=True)
            split_x(0, 1, first=True)
            w_bank(0, 1)
            t_tables()
            act.wait_ge(scales_ready, 1)
            scale_t(0, 0, first=True)
            w_bank(1, 3)
            act.wait_ge(wT_ready, 3)
            edge_tables()
            h_from_psum(0)
            q_split(0, 0)
            scale_t(0, 1, first=True)
            r_from_psum(0, 0)
            q_split(0, 1)
            r_split(0, 0, first=True)
            w_bank(3, 4)
            h_split(0, 0, first=True)
            w_bank(4, 5)
            r_from_psum(0, 1)
            h_split(0, 1, first=True)
            r_split(0, 1, first=True)
            w_bank(5, 7)
            split_x(1, 0)
            w_bank(7, 8)
            scale_t(1, 0)
            w_bank(8, 9)
            act.wait_ge(edges_ready, 1)
            y_from_psum(0, 0)
            split_x(1, 1)
            w_bank(9, 11)
            yt_out(0, 0, 0, wait=False)
            y_from_psum(0, 1)
            scale_t(1, 1)
            w_bank(11, NB)
            step(1, 1, late=True)
            with act.Fori(0, (PAIRS - 4) // 2) as k:
                step(k * 2 + 2, 0)
                step(k * 2 + 3, 1)
            step(PAIRS - 2, 0)
            step(PAIRS - 1, 1, ahead=False)
            step(PAIRS, 0, conv=False)

        @block.vector
        def _(dve):
            done = [0]

            def link(ins):
                done[0] += 1
                ins.then_inc(dve_setup, 1)
                dve.wait_ge(dve_setup, done[0])

            dve.wait_ge(modT_psum, 1)
            nc.vector.tensor_copy(condT[:], qB[:, 0:B])
            for half in range(2):
                ins = nc.vector.tensor_copy(modwT[:, :, half, :], qB[:, P:P + L * C].rearrange("p (i c) -> p i c", c=C))
            ins.then_inc(modT_ready, 1)
            dve.wait_ge(l_w, 32)
            flat = w_nat[:, :, :].rearrange("p i n -> p (i n)")
            sq = w_sq.rearrange("p a b -> p (a b)")
            link(nc.vector.tensor_tensor(sq, flat, flat, ALU.mult))
            nc.vector.tensor_reduce(w2_sum[:, :, :].rearrange("p i c -> p (i c)"),
                                    sq.rearrange("p (n k) -> p n k", k=K), AX_X, ALU.add).then_inc(w2_ready, 1)
            dve.wait_ge(modT_ready, 1)
            dve.wait_ge(s_psum, 1)
            link(nc.vector.tensor_copy(smallT[:], tB[:, 0:2 * L]))
            for i in range(L):
                ins = nc.vector.tensor_scalar(s_all[:, i, :], rB[:, B * i:B * i + B], smallT[:, i:i + 1], None, ALU.add)
            link(ins)
            nc.vector.tensor_tensor(s_sq[:], s_all[:], s_all[:], ALU.mult).then_inc(s_ready, 1)
            dve.wait_ge(w2T_psum, 1)
            nc.vector.tensor_copy(w2_sumT[:], hB[0:C, :].rearrange("p (i o) -> p i o", o=P)).then_inc(w2T_ready, 1)
            nc.vector.tensor_scalar(s0[:], s_all[:, 0, :], SCALE, None, ALU.mult).then_inc(s0_ready, 1)
            nc.vector.tensor_scalar(s2[:], s_all[:, 2, :], SCALE, None, ALU.mult)
            link(nc.vector.tensor_scalar(s3[:], s_all[:, 3, :], SCALE, None, ALU.mult))
            nc.vector.tensor_scalar(u_bias[:], s2[:], smallT[:, L + 1:L + 2], 2.0, ALU.mult, ALU.mult)
            nc.vector.tensor_scalar(v_bias[:], s3[:], smallT[:, L + 2:L + 3], None, ALU.mult)
            dve.wait_ge(pool_zero, 2)
            dve.wait_ge(w_dup_ready, 1)
            dve.wait_ge(wT_ready, 2)

            def blur_1(j):
                nc.vector.scalar_tensor_tensor(V1T[:, 3 - j:6 - j, :], wT[:, K:2 * K, 0:C], 2 * BLUR[j],
                                               V1T[:, 3 - j:6 - j, :], ALU.mult, ALU.add)
                return nc.vector.scalar_tensor_tensor(V1n[:, 3 - j:6 - j, :], w_dup[0:C, K:2 * K, 0, :], 2 * BLUR[j],
                                                      V1n[:, 3 - j:6 - j, :], ALU.mult, ALU.add)

            link(blur_1(0))
            dve.wait_ge(d_psum, 1)
            nc.vector.tensor_scalar(var[:], yB[:, 0:L * B].rearrange("p (i b) -> p i b", b=B),
                                    SCALE * SCALE, EPS, ALU.mult, ALU.add).then_inc(var_ready, 1)
            link(blur_1(1))
            link(blur_1(2))
            blur_1(3).then_inc(v1_ready, 1)
            dve.wait_ge(v1_ready, 1)
            dve.wait_ge(var_ready, 1)
            dve.wait_ge(root_ready, 1)
            link(nc.vector.reciprocal(d_all[:], rt_tmp[:]))
            dve.wait_ge(wT_ready, 3)

            def blur_3(j):
                return nc.vector.scalar_tensor_tensor(V3T[:, j:j + 3, :], wT[:, 3 * K:4 * K, 0:C], BLUR[j],
                                                      V3T[:, j:j + 3, :], ALU.mult, ALU.add)

            nc.vector.scalar_tensor_tensor(rt_tmp[:], d_all[:], -0.5, d_all[:], ALU.mult, ALU.mult)
            link(blur_3(0))
            nc.vector.tensor_tensor(rt_tmp[:], rt_tmp[:], var[:], ALU.mult)
            link(blur_3(1))
            nc.vector.scalar_tensor_tensor(d_all[:], rt_tmp[:], 1.5, d_all[:], ALU.add, ALU.mult)
            link(blur_3(2))
            nc.vector.scalar_tensor_tensor(E1[:], d_all[:, 0, :], SCALE, d_all[:, 1, :], ALU.mult, ALU.mult)
            nc.vector.tensor_tensor(b0d[:], var[:, 0, :], d_all[:, 0, :], ALU.mult)
            nc.vector.tensor_tensor(E2[:], s2[:], s_all[:, 1, :], ALU.mult)
            nc.vector.tensor_tensor(E3[:], s3[:], d_all[:, 2, :], ALU.mult)
            nc.vector.tensor_scalar(u_bias8[:], u_bias[:], BLUR[0], None, ALU.mult)
            blur_3(3).then_inc(v3_ready, 1)
            dve.wait_ge(v3_ready, 1)
            nc.vector.tensor_scalar(b0d[:], b0d[:], smallT[:, L:L + 1], None, ALU.mult).then_inc(scales_ready, 1)
            dve.wait_ge(stat_hi, 1)
            nc.vector.tensor_tensor(stat[:, LO, :, :], stat32[:], stat[:, HI, :, :].bitcast(F32), ALU.subtract).then_inc(stat_lo, 1)

            def over(tab, n, rows=slice(0, P)):
                t = tab[rows, :]
                return t.unsqueeze(1).broadcast_to([t.shape[0], n, B])

            def edge_x():
                dve.wait_ge(l_edge, 32)
                dve.wait_ge(pool_zero, 3)
                for side in range(EDGES):
                    p0 = 1 - side
                    ins = nc.vector.tensor_tensor(xs_edge[:, side, p0:p0 + 6, :],
                                                  x_edge[:, side, :, :].rearrange("p b t -> p t b"),
                                                  over(s0, 6, slice(0, C)), ALU.mult)
                ins.then_inc(xs_edge_ready, 1)

            def edge_h():
                for side in range(EDGES):
                    dve.wait_ge(he_psum, side + 1)
                    link(nc.vector.tensor_tensor(h_raw[:, side, :, :], (tB, yB)[side][:, 0:5 * B].rearrange("p (t b) -> p t b", b=B),
                                                 over(b0d, 5), ALU.add))
                    p0 = 1 - side
                    nc.vector.tensor_tensor(h_edge_s[:, side, p0:p0 + 5, :], h_raw[0:C, side, :, :],
                                            over(E1, 5, slice(0, C)), ALU.mult).then_inc(he_ready, 1)
                nc.vector.tensor_copy(h_col[0:C, 1, :], h_raw[0:C, 1, 4, :])
                nc.vector.tensor_copy(h_col[C:P, 0, :], h_raw[C:P, 0, 0, :]).then_inc(h_col_ready, 1)

            def edge_u():
                for side in range(EDGES):
                    dve.wait_ge(ue_psum, side + 1)
                    p0 = 1 - side
                    u = u_edge[:, side, p0:p0 + 4, :]
                    link(nc.vector.tensor_tensor(u, (tB, yB)[side][:, 0:4 * B].rearrange("p (t b) -> p t b", b=B),
                                                 over(E2, 4), ALU.mult))
                    link(nc.vector.tensor_tensor(u, u, over(u_bias, 4), ALU.add))
                nc.vector.tensor_tensor(u_edge[0:C, 0, 1, :], u_edge[0:C, 0, 1, :], u_bias8[0:C, :], ALU.subtract)
                nc.vector.tensor_tensor(u_edge[C:P, 1, 3, :], u_edge[C:P, 1, 3, :], u_bias8[C:P, :],
                                        ALU.subtract).then_inc(ue_ready, 1)

            def edge_v():
                dve.wait_ge(ve_psum, 1)
                for side in range(EDGES):
                    p0 = 1 - side
                    v = v_edge[:, side, p0:p0 + 3, :]
                    link(nc.vector.tensor_tensor(v, tB[:, 3 * B * side:3 * B * side + 3 * B].rearrange("p (t b) -> p t b", b=B),
                                                 over(E3, 3), ALU.mult))
                    nc.vector.tensor_tensor(v, v, over(v_bias, 3), ALU.add)
                link(nc.vector.tensor_tensor(v_int[:], tB[:, 6 * B:7 * B], E3[:], ALU.mult))
                nc.vector.tensor_tensor(v_int[:], v_int[:], v_bias[:], ALU.add).then_inc(ve_ready, 1)

            def edge_y():
                dve.wait_ge(ye_psum, 1)
                d3 = d_all[:, 3, :].unsqueeze(1).broadcast_to([P, 3, B])
                link(nc.vector.tensor_tensor(y_fix[:], yB[:, 0:3 * B].rearrange("p (t b) -> p t b", b=B), d3, ALU.mult))
                nc.vector.tensor_scalar(y_fix[:], y_fix[:], smallT[:, L + 3:L + 4], None, ALU.add).then_inc(edges_ready, 1)

            def split_x(i, a):
                dve.wait_ge(xs_hi, upto(i, a))
                nc.vector.scalar_tensor_tensor(XS[:, a, LO, :, :],
                                               X[:, a, 1:T + 1].rearrange("p (m g) -> p g m", g=4)[:, 0:3, :], col(s0, i, a),
                                               XS[:, a, HI, :, :].bitcast(F32), ALU.mult, ALU.subtract).then_inc(xs_lo, 1)

            def scale_t(i, a):
                dve.wait_ge(t_hi, upto(i, a))
                nc.vector.scalar_tensor_tensor(TT[:, a, LO, :], t_const[:, :, :].rearrange("p w o -> p (w o)"), col(E3, i, a),
                                               TT[:, a, HI, :].bitcast(F32), ALU.mult, ALU.subtract).then_inc(t_lo, 1)

            def h_from_psum(i, a):
                dve.wait_ge(h_mid, i + 1)
                n = S // 2
                nc.vector.scalar_tensor_tensor(H[:, a, 2:2 * S + 2:2].rearrange("p (m f) -> p f m", f=2),
                                               hrB[:, :, n * a:n * a + n], col(b0d, i, a),
                                               mid[:, n * a:n * a + n].unsqueeze(1).broadcast_to([P, 2, n]),
                                               ALU.add, ALU.add).then_inc(h_out, 1)

            def q_split(i, a):
                dve.wait_ge(q_hi, upto(i, a))
                nc.vector.scalar_tensor_tensor(Q[:, LO, :], qB[:, 0:5 * C], col(E2, i, a),
                                               Q[:, HI, :].bitcast(F32), ALU.mult, ALU.subtract).then_inc(q_lo, 1)

            def h_differences(i, a):
                dve.wait_ge(h_cols, upto(i, a))
                for d in range(2):
                    ins = nc.vector.tensor_tensor(H[:, a, 2 * d + 1:2 * S + 4:4], H[:, a, 4 * d:4 * d + 2 * S + 1:4],
                                                  H[:, a, 2:2 * S + 3:4], ALU.subtract)
                ins.then_inc(h_diff, 1)

            def h_split(i, a):
                dve.wait_ge(h_hi, upto(i, a))
                n = S // 2 + 1
                nc.vector.tensor_tensor(G[:, a, LO, :, 0:n], H[:, a, 1:2 * S + 5].rearrange("p (m g) -> p g m", g=4)[:, 0:3, :],
                                        G[:, a, HI, :, 0:n].bitcast(F32), ALU.subtract).then_inc(h_lo, 1)

            def r_from_psum(i, a):
                dve.wait_ge(r_psum, upto(i, a))
                if not isinstance(i, int) or i or a:
                    dve.wait_ge(r_lo, upto(i, a) - 1)
                nc.vector.tensor_scalar(R32[C:P, C:8 * C], rB[C:P, 0:7 * C], E1[C:P, bass.ds(i * 2 + a, 1)], None,
                                        ALU.mult).then_inc(r_upper, 1)
                dve.wait_ge(r_upper, upto(i, a))
                dve.wait_ge(r_lower, upto(i, a))
                r = R32[:, 0:8 * C].rearrange("p (n t c) -> p n t c", n=2, t=2)
                nc.vector.tensor_tensor(R32[:, 8 * C:12 * C].rearrange("p (n c) -> p n c", n=2), r[:, :, 0, :], r[:, :, 1, :],
                                        ALU.add).then_inc(r_sum, 1)

            def r_split(i, a):
                dve.wait_ge(r_hi, upto(i, a))
                nc.vector.tensor_tensor(RR[:, a, LO, :], R32[:], RR[:, a, HI, :].bitcast(F32), ALU.subtract).then_inc(r_lo, 1)

            def y_from_psum(i, a, first=False):
                dve.wait_ge(y_x2, upto(i, a))
                if not first:
                    dve.wait_ge(yt_psum, upto(i, a) - 2)
                nc.vector.scalar_tensor_tensor(Y[:, a, :].rearrange("p (m f) -> p f m", f=2),
                                               yB[:, :].rearrange("p (f m) -> p f m", f=2),
                                               d_all[:, 3, bass.ds(i * 2 + a, 1)],
                                               mid[:, 0:S // 2].unsqueeze(1).broadcast_to([P, 2, S // 2]),
                                               ALU.mult, ALU.add).then_inc(y_out, 1)

            def yt_out(i, a, par):
                dve.wait_ge(yt_hi, upto(i, a))
                nc.vector.tensor_tensor(YT[:, par, LO, :, C * a:C * a + C], tB[:, :].rearrange("p (c o) -> p c o", o=C),
                                        YT[:, par, HI, :, C * a:C * a + C].bitcast(F32), ALU.subtract).then_inc(yt_lo, 1)

            def route(j):
                zB = fB[0]
                dve.wait_ge(z_psum, j + 1)
                nc.vector.tensor_tensor(lg[:], zB[:, 0:E], ebias[:], ALU.add).then_inc(z_chain, 1)
                dve.wait_ge(z_chain, j * 6 + 1)
                nc.vector.tensor_reduce(lg_max[:], lg[:], AX_X, ALU.max).then_inc(z_chain, 1)
                dve.wait_ge(z_chain, j * 6 + 2)
                nc.vector.scalar_tensor_tensor(sc[:], lg[:], lg_max[:, 0:1], first_w[:], ALU.is_ge, ALU.mult).then_inc(z_chain, 1)
                dve.wait_ge(z_chain, j * 6 + 3)
                nc.vector.tensor_reduce(sc_max[:], sc[:], AX_X, ALU.max).then_inc(z_chain, 1)
                dve.wait_ge(z_chain, j * 6 + 4)
                nc.vector.scalar_tensor_tensor(zm[:, :].rearrange("p (e r) -> p e r", r=R),
                                               sc[:, :].unsqueeze(2).broadcast_to([P, E, R]), sc_max[:, 0:1],
                                               zB[:, E:GA].rearrange("p (e r) -> p e r", r=R),
                                               ALU.is_equal, ALU.mult).then_inc(z_chain, 1)
                dve.wait_ge(z_chain, j * 6 + 5)
                nc.vector.tensor_copy(zm3[:, 0::2, :], zm[:, :].unsqueeze(1).broadcast_to([P, 2, ER])).then_inc(z_chain, 1)
                dve.wait_ge(z_chain, j * 6 + 6)
                nc.vector.tensor_tensor(zm3[:, 1, :], zm[:], zm3[:, 0, :].bitcast(F32), ALU.subtract).then_inc(zm_ready, 1)

            def add(j, r, par, k, first=False):
                dve.wait_ge(f_psum, j * 3 + (r + 1))
                if r == 0:
                    dve.wait_ge(xr_landed, j * 16 + 16)
                    if not first:
                        dve.wait_ge(out_stored[par], k * 16)
                n0, n = REG[r]
                lo = max(n0, GA)
                nc.vector.tensor_tensor(OUT[:, par, lo - GA:n0 + n - GA], fB[r][:, lo - n0:n],
                                        XR[:, lo - GA:n0 + n - GA], ALU.add).then_inc(added, 1)

            def step(i, par, k, conv=True, ffn=True, ahead=True, late=False):
                kf = k - 1 + par
                if conv:
                    q_split(i, 0)
                if ffn:
                    yt_out(i - 1, 1, 1 - par)
                if conv:
                    h_from_psum(i, 0)
                    h_from_psum(i, 1)
                    h_differences(i, 0)
                    h_differences(i, 1)
                    if late:
                        late_bank(0)
                    h_split(i, 0)
                    if late:
                        late_bank(1)
                    r_from_psum(i, 0)
                    q_split(i, 1)
                    r_split(i, 0)
                    h_split(i, 1)
                    if ahead:
                        scale_t(i + 1, 0)
                    if late:
                        late_bank(2)
                    r_from_psum(i, 1)
                if ffn:
                    route(i - 1)
                if conv:
                    r_split(i, 1)
                    if late:
                        late_bank(3)
                    y_from_psum(i, 0)
                    if ahead:
                        split_x(i + 1, 0)
                        split_x(i + 1, 1)
                    yt_out(i, 0, par)
                if ffn:
                    for r in range(2):
                        add(i - 1, r, 1 - par, kf, first=isinstance(i, int) and i <= 2)
                if conv:
                    y_from_psum(i, 1)
                if ffn:
                    add(i - 1, 2, 1 - par, kf)
                if conv and ahead:
                    scale_t(i + 1, 1)

            def w_bank(n0, n1):
                for n in range(n0, n1):
                    dve.wait_ge(wt_hi, n + 1)
                    if n < NW_EARLY:
                        lo, hi = w_up_place(LO, n), w_up_place(HI, n)
                        src = fB[n % 3][:, :].rearrange("p (c o) -> p c o", o=P)
                    else:
                        lo, hi = WT[:, LO, :, 0:GA], WT[:, HI, :, 0:GA]
                        src = fB[n % 3][:, 0:CH * GA].rearrange("p (c o) -> p c o", o=GA)
                    nc.vector.tensor_tensor(lo, src, hi.bitcast(F32), ALU.subtract).then_inc(wt_lo, 1)

            def late_bank(m):
                dve.wait_ge(wt_hi, NB + m + 1)
                nc.vector.tensor_tensor(w_up_place(LO, NW_EARLY + m), fB[2][:, :].rearrange("p (c o) -> p c o", o=P),
                                        w_up_place(HI, NW_EARLY + m).bitcast(F32), ALU.subtract).then_inc(wt_lo, 1)

            split_x(0, 0)
            split_x(0, 1)
            w_bank(0, 1)
            scale_t(0, 0)
            edge_x()
            w_bank(1, 2)
            h_from_psum(0, 0)
            h_from_psum(0, 1)
            q_split(0, 0)
            w_bank(2, 3)
            scale_t(0, 1)
            edge_h()
            r_from_psum(0, 0)
            q_split(0, 1)
            h_differences(0, 0)
            r_split(0, 0)
            h_differences(0, 1)
            w_bank(3, 4)
            edge_u()
            h_split(0, 0)
            w_bank(4, 5)
            r_from_psum(0, 1)
            h_split(0, 1)
            r_split(0, 1)
            edge_v()
            w_bank(5, 7)
            edge_y()
            split_x(1, 0)
            w_bank(7, 8)
            scale_t(1, 0)
            w_bank(8, 9)
            y_from_psum(0, 0, first=True)
            split_x(1, 1)
            w_bank(9, 11)
            yt_out(0, 0, 0)
            y_from_psum(0, 1, first=True)
            scale_t(1, 1)
            w_bank(11, NW_EARLY + 1)
            dve.wait_ge(l_ga, 48)
            step(1, 1, 0, late=True)
            step(2, 0, 1)
            with dve.Fori(0, (PAIRS - 4) // 2) as k:
                step(k * 2 + 3, 1, k + 1)
                step(k * 2 + 4, 0, k + 2)
            step(PAIRS - 1, 1, PAIRS // 2 - 1, ahead=False)
            step(PAIRS, 0, PAIRS // 2, conv=False)

        @block.tensor
        def _(pe):
            pe.wait_ge(ident_ready, 1)
            pe.wait_ge(l_mod, 32)
            pe.transpose(qB[:, 0:B], cond_nat[:], ident[0:C, 0:C])
            for g in range(2):
                mm = pe.transpose(qB[:, P + P * g:2 * P + P * g], modw_nat[:, g, :], ident[:])
            mm.then_inc(modT_psum, 1)
            pe.wait_ge(l_bias, 64)
            pe.transpose(tB[:, 0:2 * L], small[:], ident[0:2 * L, 0:2 * L])
            pe.wait_ge(modT_ready, 1)
            for i in range(L):
                mm = pe.matmul(rB[:, B * i:B * i + B], modwT[:, i, :, :].rearrange("p a c -> p (a c)"), condT[:],
                               start=True, stop=True)
            mm.then_inc(s_psum, 1)

            def taps(n):
                for t in range(4):
                    mm = pe.transpose(fB[n][:, P * t:P * t + P],
                                      w_dup[:, 4 * n + t, :, :].rearrange("p a c -> p (a c)"), ident[:])
                mm.then_inc(wT_psum, 1)

            pe.wait_ge(w_dup_ready, 1)
            taps(0)
            pe.wait_ge(w2_ready, 1)
            for i in range(L):
                mm = pe.transpose(hB[0:C, P * i:P * i + P], w2_sum[:, i, :], ident[:])
            mm.then_inc(w2T_psum, 1)
            taps(1)
            pe.wait_ge(s_ready, 1)
            pe.wait_ge(w2T_ready, 1)
            for i in range(L):
                mm = pe.matmul(yB[:, B * i:B * i + B], w2_sumT[:, i, :], s_sq[0:C, i, :], start=True, stop=True)
            mm.then_inc(d_psum, 1)
            taps(2)

            def edge_h():
                pe.wait_ge(xs_edge_ready, 1)
                pe.wait_ge(h_mid, 1)
                for side in range(EDGES):
                    for k in range(K):
                        mm = pe.matmul((tB, yB)[side][:, 0:5 * B], wT[0:C, k, :], xs_edge[:, side, k:k + 5, :],
                                       start=(k == 0), stop=(k == K - 1))
                    mm.then_inc(he_psum, 1)

            def edge_u():
                for side in range(EDGES):
                    pe.wait_ge(he_ready, side + 1)
                    for k in range(3):
                        mm = pe.matmul((tB, yB)[side][:, 0:4 * B], V1n[:, 2 * k:2 * k + 2, :].rearrange("p a c -> p (a c)"),
                                       h_edge_s[:, side, 2 - k:6 - k, :], start=(k == 0), stop=(k == 2))
                    mm.then_inc(ue_psum, 1)

            def edge_v():
                pe.wait_ge(etab_ready, 1)
                pe.wait_ge(ue_ready, 1)
                for n, at in enumerate((1, 0, 2)):
                    for side in range(EDGES):
                        pe.matmul(tB[:, 3 * B * side:3 * B * side + 3 * B], v_tab[:, n, :], u_edge[:, side, at:at + 3, :],
                                  start=(n == 0 and side == 0), stop=(n == 2), skip_group_check=True)
                    mm = pe.matmul(tB[:, 6 * B:7 * B], v_tab[:, n, :], u_bias[:], start=False, stop=(n == 2),
                                   skip_group_check=True)
                mm.then_inc(ve_psum, 1)

            def edge_y():
                pe.wait_ge(ve_ready, 1)
                for j in range(4):
                    pe.matmul(yB[:, 0:2 * B], y_tab[:, j, :], v_edge[:, :, j, :], start=(j == 0), stop=(j == 3),
                              skip_group_check=True)
                    mm = pe.matmul(yB[:, 2 * B:3 * B], y_tab[:, j, :], v_int[:], start=False, stop=(j == 3),
                                   skip_group_check=True)
                mm.then_inc(ye_psum, 1)

            PASS = ((HI, HI), (HI, LO), (LO, HI))
            FP = 3 * CH

            def conv_h(i, first=False):
                pe.wait_ge(xs_lo, upto(i, 1))
                if not first:
                    pe.wait_ge(y_out, i * 2)
                for dst, tab, g in ((hB, 0, 0), (yB, 7, 1), (rB, 1, 2)):
                    for n, (w, m) in enumerate(PASS):
                        mm = pe.matmul(dst[:, :], stat[:, w, tab, :], XS[:, :, m, g, :], start=(n == 0), stop=(n == 2))
                mm.then_inc(h_psum, 1)

            def make_q(i, a, first=False):
                pe.wait_ge(t_lo, upto(i, a))
                if not first or a:
                    pe.wait_ge(q_lo, upto(i, a) - 1)
                for n, (w, m) in enumerate(PASS):
                    for t in range(2):
                        mm = pe.matmul(qB[:, C * t:C * t + 4 * C], stat[:, w, 2 + t, :], TT[:, a, m, :],
                                       start=(n == 0 and t == 0), stop=(n == 2), skip_group_check=True)
                mm.then_inc(q_psum, 1)

            def make_r(i, a):
                pe.wait_ge(q_lo, upto(i, a))
                if a:
                    pe.wait_ge(r_lower, upto(i, 0))
                    pe.wait_ge(r_upper, upto(i, 0))
                else:
                    pe.wait_ge(h_out, upto(i, 1))
                for n, (w, m) in enumerate(PASS):
                    for t in range(3):
                        mm = pe.matmul(rB[:, C * t:C * t + 5 * C], stat[:, w, 4 + t, :], Q[:, m, :],
                                       start=(n == 0 and t == 0), stop=(n == 2), skip_group_check=True)
                mm.then_inc(r_psum, 1)

            def conv_y(i, a):
                pe.wait_ge(r_lo, upto(i, a))
                pe.wait_ge(h_lo, upto(i, a))
                if a:
                    pe.wait_ge(y_out, upto(i, 0))
                N = S // 2
                for dst, taps, g in ((yB[:, 0:N], (3, 1), 0), (yB[:, N:S], (2, 0), 2), (hB[:, 0:N], (5, 4), 1)):
                    for n, (w, m) in enumerate(PASS):
                        for t in range(2):
                            mm = pe.matmul(dst, RR[:, a, w, P * taps[t]:P * taps[t] + P], G[:, a, m, g, t:t + N],
                                           start=(n == 0 and t == 0 and g != 2), stop=(n == 2 and t == 1),
                                           skip_group_check=(g != 1))
                mm.then_inc(y_psum, 1)

            def turn_y(i, a, first=False, z=True):
                pe.wait_ge(y_cols, upto(i, a))
                if not first or a:
                    pe.wait_ge(yt_lo, upto(i, a) - 1)
                if z:
                    pe.wait_ge(zt_ready, i)
                for s in range(SB):
                    mm = pe.transpose(tB[:, P * s:P * s + P], Y[:, a, P * s:P * s + P], ident[:])
                mm.then_inc(yt_psum, 1)

            def ffn(j, r, par, first_product, end, first=False):
                if first_product == 0:
                    if not first:
                        pe.wait_ge(added, j * 3 - (2 - r))
                    pe.wait_ge(yt_lo, upto(j, 1))
                n0, n = REG[r]
                for k in range(first_product, end):
                    c, (w, m) = k // 3, PASS[k % 3]
                    mm = pe.matmul(fB[r][:, 0:n], YT[:, par, w, c, :], WT[:, m, c, n0:n0 + n],
                                   start=(k == 0), stop=(k == FP - 1))
                return mm

            def turn_z(j):
                pe.wait_ge(zm_ready, j + 1)
                pe.wait_ge(yt_lo, upto(j, 1))
                pe.transpose(tB[0:3 * ER, 0:P], zm3[:, :, :].rearrange("p a z -> p (a z)").bitcast(F32),
                             ident[:]).then_inc(zt_psum, 1)

            def low_rank(j, r):
                n0, n = REG[r]
                lo = max(n0, GA)
                pe.matmul(fB[r][:, lo - n0:n], zT[:], BT[:, lo - GA:n0 + n - GA], start=False, stop=True,
                          skip_group_check=True).then_inc(f_psum, 1)

            def step(i, par, conv=True, do_ffn=True, first=False):
                ffn_first = isinstance(i, int) and i == 1
                j, q = i - 1, 1 - par
                if conv:
                    make_q(i, 0, first)
                if do_ffn:
                    turn_y(j, 1, z=False)
                if conv:
                    conv_h(i, first)
                if do_ffn:
                    if ffn_first:
                        pe.wait_ge(wt_hi, NB)
                        pe.wait_ge(wt_lo, NB - 2)
                        late_bank(0)
                    ffn(j, 0, q, 0, FP, ffn_first).then_inc(z_psum, 1)
                    if ffn_first:
                        late_bank(1)
                if conv:
                    make_r(i, 0)
                    make_q(i, 1)
                if do_ffn:
                    ffn(j, 1, q, 0, FP // 2, ffn_first)
                    if ffn_first:
                        late_bank(2)
                if conv:
                    make_r(i, 1)
                if do_ffn:
                    ffn(j, 1, q, FP // 2, FP, ffn_first)
                    if ffn_first:
                        late_bank(3)
                if conv:
                    conv_y(i, 0)
                if do_ffn:
                    turn_z(j)
                    if ffn_first:
                        pe.wait_ge(wt_lo, NB + 2)
                    ffn(j, 2, q, 0, FP // 2 + 1, ffn_first)
                    pe.wait_ge(zt_ready, i)
                    low_rank(j, 0)
                    low_rank(j, 1)
                if conv:
                    turn_y(i, 0)
                    conv_y(i, 1)
                if do_ffn:
                    ffn(j, 2, q, FP // 2 + 1, FP, ffn_first)
                    low_rank(j, 2)

            def w_up_bank(h, dst):
                ob = h // 2
                pe.wait_ge(l_wup[ob % 3], 16 * (ob // 3 + 1))
                for t in range(CH // 2):
                    c = CH // 2 * (h % 2) + t
                    t0 = 2 * P * (c // 2) + c % 2
                    mm = pe.transpose(dst[:, P * t:P * t + P], wup_nat[:, ob % 3, t0:t0 + 2 * P - 1:2], ident[:])
                return mm

            def w_bank(n0, n1):
                for n in range(n0, n1):
                    if n >= 3:
                        pe.wait_ge(wt_lo, n - 2)
                    if n < NW_EARLY:
                        mm = w_up_bank(n, fB[n % 3])
                    elif n == NW_EARLY:
                        pe.wait_ge(l_ga, 48)
                        for c in range(CH):
                            t0 = 2 * P * (c // 2) + c % 2
                            mm = pe.transpose(fB[n % 3][:, GA * c:GA * c + GA], ga_nat[:, t0:t0 + 2 * P - 1:2],
                                              ident[0:GA, 0:GA])
                    else:
                        pe.wait_ge(lb3_ready, 1)
                        for t in range(4):
                            g = 4 * (n - NW_EARLY - 1) + t
                            mm = pe.transpose(fB[n % 3][0:3 * ER, P * t:P * t + P],
                                              lb3[:, g, :, :].rearrange("p a z -> p (a z)").bitcast(F32), ident[:])
                    mm.then_inc(wt_psum, 1)

            def late_bank(m):
                if m:
                    pe.wait_ge(wt_lo, NB - 2 + m)
                w_up_bank(NW_EARLY + m, fB[2]).then_inc(wt_psum, 1)

            pe.wait_ge(wT_ready, 3)
            w_bank(0, 3)
            pe.wait_ge(stat_lo, 1)
            conv_h(0, True)
            make_q(0, 0, True)
            edge_h()
            make_r(0, 0)
            make_q(0, 1)
            w_bank(3, 5)
            edge_u()
            make_r(0, 1)
            w_bank(5, 6)
            edge_v()
            w_bank(6, 8)
            edge_y()
            w_bank(8, 9)
            pe.wait_ge(edges_ready, 1)
            conv_y(0, 0)
            w_bank(9, 11)
            turn_y(0, 0, True, z=False)
            conv_y(0, 1)
            w_bank(11, NB)
            step(1, 1)
            with pe.Fori(0, (PAIRS - 2) // 2) as k:
                step(k * 2 + 2, 0)
                step(k * 2 + 3, 1)
            step(PAIRS, 0, conv=False)


_INS = ["x", "cond_512", "L0_cond_weights", "L0_cond_biases", "L0_cond_mod_w", "L0_cond_mod_b", "L0_ffn_W_up",
        "L0_ffn_gate_w", "L0_ffn_expert_bias", "L0_ffn_lora_A", "L0_ffn_lora_B"]


def kernel(**inputs):
    import numpy as _np
    import concourse.bacc as _bacc
    from concourse import mybir as _mybir
    from concourse.bass_utils import run_bass_kernel_spmd as _run

    nc = _bacc.Bacc("TRN2", target_bir_lowering=False, num_devices=1)
    arrays, args = {}, []
    for name in _INS:
        a = _np.ascontiguousarray(inputs[name])
        arrays[f"in_{name}_dram"] = a
        args.append(nc.dram_tensor(f"in_{name}_dram", a.shape, _mybir.dt.from_np(a.dtype), kind="ExternalInput").ap())
    out = nc.dram_tensor("out_dram", inputs["x"].shape, _mybir.dt.float32, kind="ExternalOutput").ap()
    adaln_ffn_kernel(nc, *args, out)
    r = _run(nc, [arrays], core_ids=[0])
    return r.results[0]["out_dram"]
```

```python
from contextlib import ExitStack

import concourse.bass as bass
from concourse import mybir

F32 = mybir.dt.float32
F32R = mybir.dt.float32r
ALU = mybir.AluOpType
ACT = mybir.ActivationFunctionType
AX_X = mybir.AxisListType.X

P = 128
HI, LO = 0, 1


def adaln_ffn_kernel(
    nc: bass.Bass,
    x: bass.AP,
    cond: bass.AP,
    conv_w: bass.AP,
    conv_b: bass.AP,
    mod_w: bass.AP,
    mod_b: bass.AP,
    W_up: bass.AP,
    gate_w: bass.AP,
    expert_bias: bass.AP,
    lora_A: bass.AP,
    lora_B: bass.AP,
    out: bass.AP,
):
    B, C, T = x.shape
    L, _, _, K = conv_w.shape
    D = cond.shape[1]
    E = gate_w.shape[0]
    R = lora_A.shape[1]
    ER = E * R
    PAIRS = B // 2
    S = T // 2
    SB = S // P
    CH = 2 * SB
    GA = E + ER
    NW = GA + T
    SCALE = float(1.0 / (C * K) ** 0.5)
    EPS = 1e-8
    BLUR = [0.125, 0.375, 0.375, 0.125]
    M = 6
    HB = T // P
    REG = [(0, GA + 2 * P), (GA + 2 * P, 3 * P), (GA + 5 * P, 3 * P)]
    assert C == 64 and P == 2 * C and T == 1024 and D == P and L == 4 and K == 3 and NW == 1060
    EDGES = 2

    ctx = ExitStack()
    with ctx:
        def sb(name, shape, dt=F32):
            return ctx.enter_context(nc.sbuf_tensor(name, shape, dt))

        def pb(name):
            return ctx.enter_context(nc.psum_tensor(name, [P, 512], F32))

        def sem(name):
            return ctx.enter_context(nc.semaphore(name))

        ga_nat = sb("ga_nat", [GA, T])
        lb_nat = sb("lb_nat", [P, HB, E, R])
        ebias = sb("ebias", [P, E])
        ident = sb("ident", [P, P])
        smallT = sb("smallT", [P, 2 * L])
        d_all = sb("d_all", [P, L, B])
        s0 = sb("s0", [P, B])
        E1 = sb("E1", [P, B])
        E2 = sb("E2", [P, B])
        E3 = sb("E3", [P, B])
        b0d = sb("b0d", [P, B])
        h_col = sb("h_col", [P, 2, B])
        y_fix = sb("y_fix", [P, 3, B])
        stat = sb("stat", [P, 2, 8, P], F32R)
        t_const = sb("t_const", [P, 4, C])
        condT = sb("condT", [D, B])
        s_all = sb("s_all", [P, L, B])
        var = sb("var", [P, L, B])
        rt_tmp = sb("rt_tmp", [P, L, B])
        wT = sb("wT", [P, L * K, P])
        V1T = sb("V1T", [P, M, C])
        V3T = sb("V3T", [P, M, C])
        stat32 = sb("stat32", [P, 8, P])
        V1n = sb("V1n", [C, M, C])
        v_int = sb("v_int", [P, B])
        w_sq = wT[:, 0:L * C * K // P, :]
        s2 = sb("s2", [P, B])
        s3 = sb("s3", [P, B])
        u_bias = sb("u_bias", [P, B])
        u_bias8 = sb("u_bias8", [P, B])
        v_bias = sb("v_bias", [P, B])
        WT = sb("WT", [P, 2, CH, NW], F32R)
        with ExitStack() as early:
            w_nat = early.enter_context(nc.sbuf_tensor("w_nat", [P, L, C * K], F32))
            modw_nat = early.enter_context(nc.sbuf_tensor("modw_nat", [P, 2, D], F32))
            modwT = early.enter_context(nc.sbuf_tensor("modwT", [D, L, 2, C], F32))
            s_sq = early.enter_context(nc.sbuf_tensor("s_sq", [P, L, B], F32))
        BT = sb("BT", [3 * ER, T], F32R)
        lb3 = sb("lb3", [P, HB, 3, ER], F32R)
        first_w = sb("first_w", [P, E])
        X = sb("X", [P, 2, T + 2])
        XS = sb("XS", [P, 2, 2, 3, S // 2], F32R)
        H = sb("H", [P, 2, 2 * (S + 4)])
        G = sb("G", [P, 2, 2, 3, S // 2 + 2], F32R)
        TT = sb("TT", [P, 2, 2, 4 * C], F32R)
        Q = sb("Q", [P, 2, 5 * C], F32R)
        R32 = sb("R32", [P, 12 * C])
        with ExitStack() as early:
            w2_sum = early.enter_context(nc.sbuf_tensor("w2_sum", [P, L, C], F32))
            w2_sumT = early.enter_context(nc.sbuf_tensor("w2_sumT", [C, L, P], F32))
            w_dup = early.enter_context(nc.sbuf_tensor("w_dup", [P, L * K, 2, C], F32))
            cond_nat = early.enter_context(nc.sbuf_tensor("cond_nat", [C, D], F32))
            w_blur = early.enter_context(nc.sbuf_tensor("w_blur", [C, 2, K, C], F32))
            small = early.enter_context(nc.sbuf_tensor("small", [2 * L, P], F32))
        RR = sb("RR", [P, 2, 2, 12 * C], F32R)
        mid = sb("mid", [P, S + 2])
        with ExitStack() as edge:
            def tmp(name, shape, dt=F32):
                return edge.enter_context(nc.sbuf_tensor(name, shape, dt))

            x_edge = tmp("x_edge", [C, EDGES, B, 6])
            v_tab = tmp("v_tab", [P, 3, P])
            y_tab = tmp("y_tab", [P, 4, P])
            xs_edge = tmp("xs_edge", [C, EDGES, 7, B])
            h_raw = tmp("h_raw", [P, EDGES, 5, B])
            h_edge_s = tmp("h_edge_s", [C, EDGES, 6, B])
            u_edge = tmp("u_edge", [P, EDGES, 5, B])
            v_edge = tmp("v_edge", [P, EDGES, 4, B])
        Y = sb("Y", [P, 2, S])
        YT = sb("YT", [P, 2, 2, CH, P], F32R)
        rows = sb("rows", [P, 3, T])
        OUT, XR = rows[:, 0:2, :], rows[:, 2, :]
        wup_nat = rows
        lg = sb("lg", [P, E])
        lg_max = sb("lg_max", [P, 1])
        sc = sb("sc", [P, E])
        sc_max = sb("sc_max", [P, 1])
        zm = sb("zm", [P, ER])
        zm3 = sb("zm3", [P, 3, ER], F32R)
        zT = sb("zT", [3 * ER, P], F32R)

        hrB = ctx.enter_context(nc.psum_tensor("hrB", [P, 2, 512], F32))
        hB, rB = hrB[:, 0, :], hrB[:, 1, :]
        ytB = ctx.enter_context(nc.psum_tensor("ytB", [P, 1024], F32))
        yB, tB = ytB[:, 0:512], ytB[:, 512:1024]
        qB = pb("qB")
        fB = [pb("zB"), pb("f1B"), pb("f2B")]

        l_mod = sem("l_mod")
        l_w = sem("l_w")
        l_bias = sem("l_bias")
        l_edge = sem("l_edge")
        l_wup = [sem(f"l_wup{n}") for n in range(3)]
        l_ga = sem("l_ga")
        l_lb = sem("l_lb")
        ident_ready = sem("ident_ready")
        pool_zero = sem("pool_zero")
        dve_setup = sem("dve_setup")
        modT_psum = sem("modT_psum")
        modT_ready = sem("modT_ready")
        s_psum = sem("s_psum")
        s_ready = sem("s_ready")
        w2_ready = sem("w2_ready")
        w2T_psum = sem("w2T_psum")
        w2T_ready = sem("w2T_ready")
        w_dup_ready = sem("w_dup_ready")
        wT_psum = sem("wT_psum")
        wT_ready = sem("wT_ready")
        d_psum = sem("d_psum")
        var_ready = sem("var_ready")
        root_ready = sem("root_ready")
        l0_tables = sem("l0_tables")
        l0_sum = sem("l0_sum")
        s0_ready = sem("s0_ready")
        scales_ready = sem("scales_ready")
        v1_ready = sem("v1_ready")
        v1n_ready = sem("v1n_ready")
        v3_ready = sem("v3_ready")
        act_tables = sem("act_tables")
        stat_hi = sem("stat_hi")
        stat_lo = sem("stat_lo")
        stat_lo_qr = sem("stat_lo_qr")
        xs_edge_ready = sem("xs_edge_ready")
        he_psum = sem("he_psum")
        he_ready = sem("he_ready")
        h_col_ready = sem("h_col_ready")
        ue_psum = sem("ue_psum")
        ue_ready = sem("ue_ready")
        ve_psum = sem("ve_psum")
        ve_ready = sem("ve_ready")
        ye_psum = sem("ye_psum")
        edges_ready = sem("edges_ready")
        etab_ready = sem("etab_ready")
        lb3_ready = sem("lb3_ready")
        wt_psum = sem("wt_psum")
        wt_hi = sem("wt_hi")
        wt_lo = sem("wt_lo")
        x_landed = sem("x_landed")
        xr_landed = sem("xr_landed")
        out_stored = [sem(f"out_stored{p}") for p in range(2)]
        x_diff, h_x2, h_psum, h_mid, h_cols = sem("x_diff"), sem("h_x2"), sem("h_psum"), sem("h_mid"), sem("h_cols")
        xs_hi, xs_lo = sem("xs_hi"), sem("xs_lo")
        t_hi, t_lo = sem("t_hi"), sem("t_lo")
        h_out, h_diff = sem("h_out"), sem("h_diff")
        h_hi, h_lo = sem("h_hi"), sem("h_lo")
        q_psum, q_hi, q_lo = sem("q_psum"), sem("q_hi"), sem("q_lo")
        r_psum, r_lower, r_upper, r_sum = sem("r_psum"), sem("r_lower"), sem("r_upper"), sem("r_sum")
        r_hi, r_lo = sem("r_hi"), sem("r_lo")
        y_x2, y_psum, y_mid, y_out, y_cols = sem("y_x2"), sem("y_psum"), sem("y_mid"), sem("y_out"), sem("y_cols")
        yt_psum, yt_hi, yt_lo = sem("yt_psum"), sem("yt_hi"), sem("yt_lo")
        z_psum = sem("z_psum")
        z_chain = sem("z_chain")
        zm_ready = sem("zm_ready")
        zt_psum = sem("zt_psum")
        zt_ready = sem("zt_ready")
        f_psum = sem("f_psum")
        added = sem("added")

        GA_BANK = 6
        LATE = 6
        LATE_PLACE = (2, 1, 2, 1, 2, 2)
        NB = 2 * HB - LATE + 3

        def half_of(n):
            return n if n < GA_BANK else n - 3

        def banks_to(block):
            return 2 * block + 2 + (0 if 2 * block < GA_BANK else 3)

        def upto(i, a):
            return i * 2 + (a + 1)

        def w_up_place(part, h):
            c0, o0 = CH // 2 * (h % 2), GA + P * (h // 2)
            return WT[:, part, c0:c0 + CH // 2, o0:o0 + P]

        def col(tab, i, a):
            return tab[:, bass.ds(i * 2 + a, 1)]

        x_conv = x.rearrange("(i a) c t -> i c a t", a=2)
        x_rows = x.rearrange("(i a) c t -> i (a c) t", a=2)
        out_rows = out.rearrange("(i a) c t -> i (a c) t", a=2)

        block = ctx.enter_context(nc.Block())

        @block.sync
        def _(sp):
            sp.dma_start(cond_nat[:], cond).then_inc(l_mod, 16)
            sp.dma_start(modw_nat[:], mod_w.rearrange("i c d -> (i c) d").rearrange("(g p) d -> p g d", p=P)).then_inc(l_mod, 16)
            for n, rows in enumerate((mod_b, conv_b)):
                sp.dma_start(small[L * n:L * n + L, :].rearrange("i (a c) -> i a c", a=2),
                             rows.unsqueeze(1).broadcast_to([L, 2, C])).then_inc(l_bias, 16)
            for half in range(2):
                sp.dma_start(w_nat[C * half:C * half + C, :, :],
                             conv_w.rearrange("i o c k -> o i (c k)")).then_inc(l_w, 16)

            def load_x(i):
                sp.dma_start(X[0:C, :, 2:T + 2], x_conv[i]).then_inc(x_landed, 16)
                sp.dma_start(X[C:P, :, 1:T + 1], x_conv[i]).then_inc(x_landed, 16)

            load_x(0)
            sp.dma_start(wup_nat[:, 0, :], W_up[0:P, :]).then_inc(l_wup[0], 16)
            sp.dma_start(x_edge[:, 0, :, :], x[:, :, 0:6].rearrange("b c t -> c b t")).then_inc(l_edge, 16)
            sp.dma_start(x_edge[:, 1, :, :], x[:, :, T - 6:T].rearrange("b c t -> c b t")).then_inc(l_edge, 16)
            for n in range(1, 3):
                sp.dma_start(wup_nat[:, n, :], W_up[P * n:P * n + P, :]).then_inc(l_wup[n], 16)
            sp.dma_start(ebias[:], expert_bias.partition_broadcast(P)).then_inc(l_ga, 16)
            sp.dma_start(ga_nat[0:E, :], gate_w).then_inc(l_ga, 16)
            sp.dma_start(ga_nat[E:GA, :], lora_A.rearrange("e r h -> (e r) h")).then_inc(l_ga, 16)
            for e in range(E):
                sp.dma_start(lb_nat[:, :, e, :], lora_B[e].rearrange("(g p) r -> p g r", p=P)).then_inc(l_lb, 16)
            for n in range(3, HB):
                sp.wait_ge(wt_psum, banks_to(n - 3))
                sp.dma_start(wup_nat[:, n % 3, :], W_up[P * n:P * n + P, :]).then_inc(l_wup[n % 3], 16)
                if n == 3:
                    sp.wait_ge(xs_lo, 2)
                    load_x(1)

            def step(i, par, load=True, xr=True, store=True):
                if load:
                    sp.wait_ge(xs_lo, upto(i + 1, 1))
                    load_x(i + 2)
                if store:
                    sp.wait_ge(added, i * 3)
                    sp.dma_start(out_rows[i - 1], OUT[:, 1 - par, :]).then_inc(out_stored[1 - par], 16)
                if xr:
                    sp.dma_start(XR, x_rows[i]).then_inc(xr_landed, 16)

            sp.wait_ge(wt_psum, banks_to(HB - 3))
            step(0, 0, store=False)
            step(1, 1)
            with sp.Fori(0, (PAIRS - 4) // 2) as k:
                step(k * 2 + 2, 0)
                step(k * 2 + 3, 1)
            step(PAIRS - 2, 0, load=False)
            step(PAIRS - 1, 1, load=False)
            cut = REG[2][0] - GA
            for n, cols in ((2, slice(0, cut)), (3, slice(cut, T))):
                sp.wait_ge(added, (PAIRS - 1) * 3 + n)
                sp.dma_start(out_rows[PAIRS - 1][:, cols], OUT[:, 1, cols]).then_inc(out_stored[1], 16)
            sp.wait_ge(out_stored[0], 16 * (PAIRS // 2))
            sp.wait_ge(out_stored[1], 16 * (PAIRS // 2 + 1))

        @block.gpsimd
        def _(pool):
            nc.gpsimd.memset(ident[:], 0.0).then_inc(pool_zero, 1)
            pool.wait_ge(pool_zero, 1)
            nc.gpsimd.affine_select(out=ident[:], in_=ident[:], compare_op=ALU.not_equal, fill=1.0,
                                    base=0, pattern=[[-1, P]], channel_multiplier=1).then_inc(ident_ready, 1)
            nc.gpsimd.memset(V1n[:], 0.0)
            nc.gpsimd.memset(V1T[:], 0.0)
            nc.gpsimd.memset(V3T[:], 0.0)
            nc.gpsimd.memset(stat32[:], 0.0)
            nc.gpsimd.memset(t_const[:], 0.0).then_inc(pool_zero, 1)
            nc.gpsimd.memset(X[:, :, 0:1], 0.0)
            nc.gpsimd.memset(xs_edge[:], 0.0)
            nc.gpsimd.memset(h_edge_s[:], 0.0)
            nc.gpsimd.memset(u_edge[:], 0.0)
            nc.gpsimd.memset(v_edge[:], 0.0)
            nc.gpsimd.memset(v_tab[:], 0.0)
            nc.gpsimd.memset(y_tab[:], 0.0)
            nc.gpsimd.memset(h_col[:], 0.0)
            nc.gpsimd.memset(H[:, :, 0:1], 0.0)
            nc.gpsimd.memset(H[:, :, 2 * S + 4:2 * S + 8], 0.0)
            nc.gpsimd.memset(R32[:], 0.0)
            for e in range(E):
                ins = nc.gpsimd.memset(first_w[:, e:e + 1], float(E - e))
            ins.then_inc(pool_zero, 1)

            def x_differences(i):
                pool.wait_ge(x_landed, i * 32 + 32)
                for d in range(2):
                    ins = nc.gpsimd.tensor_tensor(X[:, :, 2 * d + 1:T:4], X[:, :, 4 * d:4 * d + T - 3:4], X[:, :, 2:T:4],
                                                  ALU.subtract)
                ins.then_inc(x_diff, 1)

            def y_columns(i, a, first=False):
                if not first:
                    pool.wait_ge(yt_psum, upto(i, a) - 2)
                nc.gpsimd.tensor_copy(Y[:, a, 0:S:S - 1].unsqueeze(2),
                                      y_fix[:, 0:2, bass.ds(i * 2 + a, 1)]).then_inc(y_cols, 1)

            def step(i, ahead=True):
                for a in range(2):
                    y_columns(i, a)
                if ahead:
                    x_differences(i + 1)

            pool.wait_ge(pool_zero, 3)
            x_differences(0)
            pool.wait_ge(l0_tables, 1)
            nc.gpsimd.tensor_tensor(stat32[:, 7, :], stat32[:, 0, :], stat32[:, 1, :], ALU.add).then_inc(l0_sum, 1)
            pool.wait_ge(l_edge, 32)
            pool.wait_ge(s0_ready, 1)
            for side in range(EDGES):
                p0 = 1 - side
                ins = nc.gpsimd.tensor_tensor(xs_edge[:, side, p0:p0 + 6, :], x_edge[:, side, :, :].rearrange("p b t -> p t b"),
                                              s0[0:C, :].unsqueeze(1).broadcast_to([C, 6, B]), ALU.mult)
            ins.then_inc(xs_edge_ready, 1)
            pool.wait_ge(stat_hi, 1)
            nc.gpsimd.tensor_tensor(stat[:, LO, 2:7, :], stat32[:, 2:7, :], stat[:, HI, 2:7, :].bitcast(F32),
                                    ALU.subtract).then_inc(stat_lo_qr, 1)
            pool.wait_ge(w_dup_ready, 1)
            for n in range(2):
                ins = nc.gpsimd.tensor_scalar(w_blur[:, n, :, :], w_dup[0:C, K:2 * K, 0, :], 2 * BLUR[n], None, ALU.mult)
            ins.then_inc(v1n_ready, 1)
            pool.wait_ge(v1n_ready, 1)
            for j in range(4):
                nc.gpsimd.tensor_tensor(V1n[:, 3 - j:6 - j, :], V1n[:, 3 - j:6 - j, :], w_blur[:, min(j, 3 - j), :, :],
                                        ALU.add).then_inc(v1n_ready, 1)
                pool.wait_ge(v1n_ready, j + 2)
            pool.wait_ge(l_lb, 64)
            pool.wait_ge(var_ready, 1)
            lb = lb_nat[:, :, :, :].rearrange("p g e r -> p g (e r)")
            nc.gpsimd.tensor_copy(lb3[:, :, 0, :], lb)
            nc.gpsimd.tensor_copy(lb3[:, :, 1, :], lb).then_inc(pool_zero, 1)
            pool.wait_ge(pool_zero, 4)
            nc.gpsimd.tensor_tensor(lb3[:, :, 2, :], lb, lb3[:, :, 0, :].bitcast(F32), ALU.subtract).then_inc(lb3_ready, 1)
            x_differences(1)
            for a in range(2):
                pool.wait_ge(h_hi, upto(0, a))
                n = S // 2 + 1
                nc.gpsimd.tensor_tensor(G[:, a, LO, :, 0:n], H[:, a, 1:2 * S + 5].rearrange("p (m g) -> p g m", g=4)[:, 0:3, :],
                                        G[:, a, HI, :, 0:n].bitcast(F32), ALU.subtract).then_inc(h_lo, 1)
            pool.wait_ge(edges_ready, 1)
            for a in range(2):
                y_columns(0, a, first=True)
            with pool.Fori(1, PAIRS - 1) as i:
                step(i)
            step(PAIRS - 1, ahead=False)

        @block.scalar
        def _(act):
            act.wait_ge(ident_ready, 1)
            nc.scalar.activation(mid[:, 0:1], ident[:, 0:1], ACT.Sqrt)
            wv = w_nat[:, :, :].rearrange("p i (c k) -> p i k c", k=K)
            act.wait_ge(l_w, 32)
            for i in range(L):
                ins = nc.scalar.activation(w_dup[:, K * i:K * i + K, :, :],
                                           wv[:, i, :, :].unsqueeze(2).broadcast_to([P, K, 2, C]), ACT.Copy)
            ins.then_inc(w_dup_ready, 1)
            act.wait_ge(w_dup_ready, 1)

            def taps(n):
                act.wait_ge(wT_psum, n + 1)
                if n == 0:
                    act.wait_ge(w2_ready, 1)
                nc.scalar.activation(wT[:, 4 * n:4 * n + 4, :], fB[n][:, :].rearrange("p (t o) -> p t o", o=P),
                                     ACT.Copy).then_inc(wT_ready, 1)

            T0, T2 = 0, 2 * K
            act.wait_ge(pool_zero, 2)
            for r0, c0, tab, tap in ((0, 0, 2, 2), (C, 0, 2, 1), (C, C, 2, 2), (0, 0, 3, 0), (0, C, 3, 1), (C, C, 3, 0)):
                nc.scalar.activation(stat32[r0:r0 + C, tab, c0:c0 + C], w_dup[r0:r0 + C, T2 + tap, 0, :], ACT.Copy)
            taps(0)
            act.wait_ge(w2T_psum, 1)
            nc.scalar.activation(w2_sumT[:], hB[0:C, :].rearrange("p (i o) -> p i o", o=P), ACT.Copy).then_inc(w2T_ready, 1)
            taps(1)
            act.wait_ge(wT_ready, 1)
            for r0, c0, tab, tap in ((0, 0, 0, 0), (C, 0, 0, 1), (C, C, 0, 0), (0, 0, 1, 2), (0, C, 1, 1), (C, C, 1, 2)):
                ins = nc.scalar.activation(stat32[r0:r0 + C, tab, c0:c0 + C], wT[r0:r0 + C, T0 + tap, c0:c0 + C], ACT.Copy)
            ins.then_inc(l0_tables, 1)
            act.wait_ge(var_ready, 1)
            nc.scalar.activation(rt_tmp[:], var[:], ACT.Sqrt).then_inc(root_ready, 1)
            taps(2)
            act.wait_ge(v1_ready, 1)
            for e in range(2):
                r = slice(C * e, C * e + C)
                ins = nc.scalar.activation(stat32[r, 4:7, :].rearrange("p t (a c) -> p t a c", a=2),
                                           V1T[r, e::2, :].unsqueeze(2).broadcast_to([C, 3, 2, C]), ACT.Copy)
            ins.then_inc(act_tables, 1)

            def t_tables():
                act.wait_ge(v3_ready, 1)
                for w in range(3):
                    nc.scalar.activation(t_const[0:C, w, :], V3T[0:C, 5 - 2 * w, :], ACT.Copy)
                    ins = nc.scalar.activation(t_const[C:P, w + 1, :], V3T[C:P, 4 - 2 * w, :], ACT.Copy)
                ins.then_inc(act_tables, 1)
                act.wait_ge(act_tables, 2)

            def v_table():
                act.wait_ge(pool_zero, 3)
                for r0, c0, tab, tap in ((0, 0, 0, 1), (0, C, 0, 0), (C, 0, 0, 2), (C, C, 0, 1), (C, 0, 1, 0), (0, C, 2, 2)):
                    ins = nc.scalar.activation(v_tab[r0:r0 + C, tab, c0:c0 + C], wT[r0:r0 + C, T2 + tap, c0:c0 + C], ACT.Copy)
                ins.then_inc(etab_ready, 1)

            def y_table():
                for e in range(2):
                    r = slice(C * e, C * e + C)
                    nc.scalar.activation(y_tab[r, 0:3, 0:C], V3T[r, e::2, :], ACT.Copy)
                    ins = nc.scalar.activation(y_tab[r, 1:4, C:P], V3T[r, e::2, :], ACT.Copy)
                ins.then_inc(etab_ready, 1)

            def split_x(i, a, first=False):
                act.wait_ge(x_diff, i + 1)
                if not first:
                    act.wait_ge(h_psum, i)
                nc.scalar.activation(XS[:, a, HI, :, :], X[:, a, 1:T + 1].rearrange("p (m g) -> p g m", g=4)[:, 0:3, :],
                                     ACT.Copy, scale=col(s0, i, a)).then_inc(xs_hi, 1)

            def scale_t(i, a, first=False):
                if not first:
                    act.wait_ge(q_psum, upto(i, a) - 2)
                nc.scalar.activation(TT[:, a, HI, :], t_const[:], ACT.Copy, scale=col(E3, i, a)).then_inc(t_hi, 1)

            def h_from_psum(i):
                act.wait_ge(h_x2, i + 1)
                nc.scalar.activation(mid[:, 0:S], yB[:], ACT.Copy).then_inc(h_mid, 1)

            def q_split(i, a):
                act.wait_ge(q_psum, upto(i, a))
                if not isinstance(i, int) or i or a:
                    act.wait_ge(r_psum, upto(i, a) - 1)
                nc.scalar.activation(Q[:, HI, :], qB[:, 0:5 * C], ACT.Copy, scale=col(E2, i, a)).then_inc(q_hi, 1)

            def h_split(i, a, first=False):
                act.wait_ge(h_diff, upto(i, a))
                if not first:
                    act.wait_ge(y_psum, upto(i, a) - 2)
                nc.scalar.activation(G[:, a, HI, :, 0:S // 2 + 1],
                                     H[:, a, 1:2 * S + 5].rearrange("p (m g) -> p g m", g=4)[:, 0:3, :],
                                     ACT.Copy).then_inc(h_hi, 1)

            def r_from_psum(i, a):
                act.wait_ge(r_psum, upto(i, a))
                if not isinstance(i, int) or i or a:
                    act.wait_ge(r_lo, upto(i, a) - 1)
                nc.scalar.activation(R32[0:C, 0:7 * C], rB[0:C, 0:7 * C], ACT.Copy,
                                     scale=E1[0:C, bass.ds(i * 2 + a, 1)]).then_inc(r_lower, 1)

            def r_split(i, a, first=False):
                act.wait_ge(r_sum, upto(i, a))
                if not first:
                    act.wait_ge(y_psum, upto(i, a) - 2)
                nc.scalar.activation(RR[:, a, HI, :], R32[:], ACT.Copy).then_inc(r_hi, 1)

            def y_from_psum(i, a):
                act.wait_ge(y_x2, upto(i, a))
                if a:
                    act.wait_ge(y_out, upto(i, 0))
                nc.scalar.activation(mid[:, 0:S].rearrange("p (f m) -> p f m", f=2),
                                     hB[:, 0:S // 2].unsqueeze(1).broadcast_to([P, 2, S // 2]), ACT.Identity,
                                     scale=d_all[:, 3, bass.ds(i * 2 + a, 1)],
                                     bias=y_fix[:, 2, bass.ds(i * 2 + a, 1)]).then_inc(y_mid, 1)

            def yt_out(i, a, par, wait=True):
                act.wait_ge(yt_psum, upto(i, a))
                if wait:
                    act.wait_ge(f_psum, i * 3 - 3)
                nc.scalar.activation(YT[:, par, HI, :, C * a:C * a + C],
                                     tB[:, :].rearrange("p (c o) -> p c o", o=C), ACT.Copy).then_inc(yt_hi, 1)

            def step(i, par, conv=True, ahead=True, late=False):
                wait = not (isinstance(i, int) and i < 2)
                if conv:
                    q_split(i, 0)
                    h_from_psum(i)
                    if late:
                        late_bank(0)
                        late_bank(1)
                    h_split(i, 0)
                    if late:
                        late_bank(2)
                        late_bank(3)
                    r_from_psum(i, 0)
                    q_split(i, 1)
                    if late:
                        late_bank(4)
                    r_split(i, 0)
                    h_split(i, 1)
                    if ahead:
                        scale_t(i + 1, 0)
                    r_from_psum(i, 1)
                    y_from_psum(i, 0)
                    r_split(i, 1)
                    yt_out(i, 0, par, wait)
                    if late:
                        late_bank(5)
                    if ahead:
                        split_x(i + 1, 0)
                    y_from_psum(i, 1)
                    if ahead:
                        split_x(i + 1, 1)
                act.wait_ge(zt_psum, i)
                nc.scalar.activation(zT[:], tB[0:3 * ER, 0:P], ACT.Copy).then_inc(zt_ready, 1)
                if conv:
                    yt_out(i, 1, par, wait)
                    if ahead:
                        scale_t(i + 1, 1)

            def w_bank(n0, n1):
                for n in range(n0, n1):
                    act.wait_ge(wt_psum, n + 1)
                    if n == GA_BANK:
                        dst, src = WT[:, HI, :, 0:GA], fB[n % 3][:, 0:CH * GA].rearrange("p (c o) -> p c o", o=GA)
                    elif n in (GA_BANK + 1, GA_BANK + 2):
                        h0 = 512 * (n - GA_BANK - 1)
                        dst, src = BT[:, h0:h0 + 512], fB[n % 3][0:3 * ER, :]
                    else:
                        dst, src = w_up_place(HI, half_of(n)), fB[n % 3][:, :].rearrange("p (c o) -> p c o", o=P)
                    nc.scalar.activation(dst, src, ACT.Copy).then_inc(wt_hi, 1)

            def late_bank(m):
                act.wait_ge(wt_psum, NB + m + 1)
                nc.scalar.activation(w_up_place(HI, half_of(NB + m)), fB[LATE_PLACE[m]][:, :].rearrange("p (c o) -> p c o", o=P),
                                     ACT.Copy).then_inc(wt_hi, 1)

            act.wait_ge(pool_zero, 3)
            act.wait_ge(act_tables, 1)
            act.wait_ge(l0_sum, 1)
            nc.scalar.activation(stat[:, HI, :, :], stat32[:], ACT.Copy).then_inc(stat_hi, 1)
            act.wait_ge(s0_ready, 1)
            split_x(0, 0, first=True)
            split_x(0, 1, first=True)
            w_bank(0, 1)
            act.wait_ge(wT_ready, 3)
            v_table()
            t_tables()
            act.wait_ge(scales_ready, 1)
            scale_t(0, 0, first=True)
            w_bank(1, 3)
            h_from_psum(0)
            q_split(0, 0)
            scale_t(0, 1, first=True)
            y_table()
            r_from_psum(0, 0)
            q_split(0, 1)
            h_split(0, 0, first=True)
            r_split(0, 0, first=True)
            w_bank(3, 4)
            h_split(0, 1, first=True)
            r_from_psum(0, 1)
            r_split(0, 1, first=True)
            w_bank(4, 5)
            act.wait_ge(edges_ready, 1)
            y_from_psum(0, 0)
            w_bank(5, 7)
            yt_out(0, 0, 0, wait=False)
            split_x(1, 0)
            w_bank(7, 10)
            split_x(1, 1)
            y_from_psum(0, 1)
            scale_t(1, 0)
            w_bank(10, 11)
            scale_t(1, 1)
            w_bank(11, NB)
            yt_out(0, 1, 0, wait=False)
            step(1, 1, late=True)
            with act.Fori(0, (PAIRS - 4) // 2) as k:
                step(k * 2 + 2, 0)
                step(k * 2 + 3, 1)
            step(PAIRS - 2, 0)
            step(PAIRS - 1, 1, ahead=False)
            step(PAIRS, 0, conv=False)

        @block.vector
        def _(dve):
            done = [0]

            def link(ins):
                done[0] += 1
                ins.then_inc(dve_setup, 1)
                dve.wait_ge(dve_setup, done[0])

            dve.wait_ge(modT_psum, 1)
            nc.vector.tensor_copy(condT[:], qB[:, 0:B])
            for half in range(2):
                ins = nc.vector.tensor_copy(modwT[:, :, half, :], qB[:, P:P + L * C].rearrange("p (i c) -> p i c", c=C))
            ins.then_inc(modT_ready, 1)
            dve.wait_ge(l_w, 32)
            flat = w_nat[:, :, :].rearrange("p i n -> p (i n)")
            sq = w_sq.rearrange("p a b -> p (a b)")
            link(nc.vector.tensor_tensor(sq, flat, flat, ALU.mult))
            nc.vector.tensor_reduce(w2_sum[:, :, :].rearrange("p i c -> p (i c)"),
                                    sq.rearrange("p (n k) -> p n k", k=K), AX_X, ALU.add).then_inc(w2_ready, 1)
            dve.wait_ge(modT_ready, 1)
            dve.wait_ge(s_psum, 1)
            link(nc.vector.tensor_copy(smallT[:], tB[:, 0:2 * L]))
            for i in range(L):
                ins = nc.vector.tensor_scalar(s_all[:, i, :], rB[:, B * i:B * i + B], smallT[:, i:i + 1], None, ALU.add)
            link(ins)
            nc.vector.tensor_tensor(s_sq[:], s_all[:], s_all[:], ALU.mult).then_inc(s_ready, 1)
            nc.vector.tensor_scalar(s0[:], s_all[:, 0, :], SCALE, None, ALU.mult).then_inc(s0_ready, 1)
            nc.vector.tensor_scalar(s2[:], s_all[:, 2, :], SCALE, None, ALU.mult)
            link(nc.vector.tensor_scalar(s3[:], s_all[:, 3, :], SCALE, None, ALU.mult))
            nc.vector.tensor_scalar(u_bias[:], s2[:], smallT[:, L + 1:L + 2], 2.0, ALU.mult, ALU.mult)
            nc.vector.tensor_scalar(v_bias[:], s3[:], smallT[:, L + 2:L + 3], None, ALU.mult)
            dve.wait_ge(pool_zero, 2)
            dve.wait_ge(wT_ready, 2)

            def blur_1(j):
                return nc.vector.scalar_tensor_tensor(V1T[:, 3 - j:6 - j, :], wT[:, K:2 * K, 0:C], 2 * BLUR[j],
                                                      V1T[:, 3 - j:6 - j, :], ALU.mult, ALU.add)

            link(blur_1(0))
            dve.wait_ge(d_psum, 1)
            nc.vector.tensor_scalar(var[:], yB[:, 0:L * B].rearrange("p (i b) -> p i b", b=B),
                                    SCALE * SCALE, EPS, ALU.mult, ALU.add).then_inc(var_ready, 1)
            link(blur_1(1))
            link(blur_1(2))
            blur_1(3).then_inc(v1_ready, 1)
            dve.wait_ge(v1_ready, 1)
            dve.wait_ge(var_ready, 1)
            dve.wait_ge(root_ready, 1)
            link(nc.vector.reciprocal(d_all[:], rt_tmp[:]))
            def over(tab, n, rows=slice(0, P)):
                t = tab[rows, :]
                return t.unsqueeze(1).broadcast_to([t.shape[0], n, B])

            def edge_h():
                dve.wait_ge(scales_ready, 1)
                for side in range(EDGES):
                    dve.wait_ge(he_psum, side + 1)
                    link(nc.vector.tensor_tensor(h_raw[:, side, :, :], (tB, qB)[side][:, 0:5 * B].rearrange("p (t b) -> p t b", b=B),
                                                 over(b0d, 5), ALU.add))
                    p0 = 1 - side
                    nc.vector.tensor_tensor(h_edge_s[:, side, p0:p0 + 5, :], h_raw[0:C, side, :, :],
                                            over(E1, 5, slice(0, C)), ALU.mult).then_inc(he_ready, 1)
                nc.vector.tensor_copy(h_col[0:C, 1, :], h_raw[0:C, 1, 4, :])
                nc.vector.tensor_copy(h_col[C:P, 0, :], h_raw[C:P, 0, 0, :]).then_inc(h_col_ready, 1)

            def edge_u():
                for side in range(EDGES):
                    dve.wait_ge(ue_psum, side + 1)
                    p0 = 1 - side
                    u = u_edge[:, side, p0:p0 + 4, :]
                    link(nc.vector.tensor_tensor(u, (tB, yB)[side][:, 0:4 * B].rearrange("p (t b) -> p t b", b=B),
                                                 over(E2, 4), ALU.mult))
                    link(nc.vector.tensor_tensor(u, u, over(u_bias, 4), ALU.add))
                nc.vector.tensor_tensor(u_edge[0:C, 0, 1, :], u_edge[0:C, 0, 1, :], u_bias8[0:C, :], ALU.subtract)
                nc.vector.tensor_tensor(u_edge[C:P, 1, 3, :], u_edge[C:P, 1, 3, :], u_bias8[C:P, :],
                                        ALU.subtract).then_inc(ue_ready, 1)

            def edge_v():
                dve.wait_ge(ve_psum, 1)
                for side in range(EDGES):
                    p0 = 1 - side
                    v = v_edge[:, side, p0:p0 + 3, :]
                    link(nc.vector.tensor_tensor(v, tB[:, 3 * B * side:3 * B * side + 3 * B].rearrange("p (t b) -> p t b", b=B),
                                                 over(E3, 3), ALU.mult))
                    nc.vector.tensor_tensor(v, v, over(v_bias, 3), ALU.add)
                link(nc.vector.tensor_tensor(v_int[:], tB[:, 6 * B:7 * B], E3[:], ALU.mult))
                nc.vector.tensor_tensor(v_int[:], v_int[:], v_bias[:], ALU.add).then_inc(ve_ready, 1)

            def edge_y():
                dve.wait_ge(ye_psum, 1)
                d3 = d_all[:, 3, :].unsqueeze(1).broadcast_to([P, 3, B])
                link(nc.vector.tensor_tensor(y_fix[:], tB[:, 0:3 * B].rearrange("p (t b) -> p t b", b=B), d3, ALU.mult))
                nc.vector.tensor_scalar(y_fix[:], y_fix[:], smallT[:, L + 3:L + 4], None, ALU.add).then_inc(edges_ready, 1)

            def split_x(i, a):
                dve.wait_ge(xs_hi, upto(i, a))
                nc.vector.scalar_tensor_tensor(XS[:, a, LO, :, :],
                                               X[:, a, 1:T + 1].rearrange("p (m g) -> p g m", g=4)[:, 0:3, :], col(s0, i, a),
                                               XS[:, a, HI, :, :].bitcast(F32), ALU.mult, ALU.subtract).then_inc(xs_lo, 1)

            def scale_t(i, a):
                dve.wait_ge(t_hi, upto(i, a))
                nc.vector.scalar_tensor_tensor(TT[:, a, LO, :], t_const[:, :, :].rearrange("p w o -> p (w o)"), col(E3, i, a),
                                               TT[:, a, HI, :].bitcast(F32), ALU.mult, ALU.subtract).then_inc(t_lo, 1)

            def h_from_psum(i, a):
                dve.wait_ge(h_psum, i + 1)
                dve.wait_ge(h_mid, i + 1)
                n = S // 2
                nc.vector.scalar_tensor_tensor(H[:, a, 2:2 * S + 2:2].rearrange("p (m f) -> p f m", f=2),
                                               hrB[:, :, n * a:n * a + n], col(b0d, i, a),
                                               mid[:, n * a:n * a + n].unsqueeze(1).broadcast_to([P, 2, n]),
                                               ALU.add, ALU.add).then_inc(h_out, 1)

            def q_split(i, a):
                dve.wait_ge(q_hi, upto(i, a))
                nc.vector.scalar_tensor_tensor(Q[:, LO, :], qB[:, 0:5 * C], col(E2, i, a),
                                               Q[:, HI, :].bitcast(F32), ALU.mult, ALU.subtract).then_inc(q_lo, 1)

            def h_columns(i):
                dve.wait_ge(h_out, upto(i, 1))
                nc.vector.tensor_copy(H[:, :, 2:2 * S + 3:2 * S],
                                      h_col[:, :, bass.ds(i * 2, 2)].rearrange("p e a -> p a e")).then_inc(h_cols, 1)

            def h_differences(i, a):
                dve.wait_ge(h_cols, i + 1)
                for d in range(2):
                    ins = nc.vector.tensor_tensor(H[:, a, 2 * d + 1:2 * S + 4:4], H[:, a, 4 * d:4 * d + 2 * S + 1:4],
                                                  H[:, a, 2:2 * S + 3:4], ALU.subtract)
                ins.then_inc(h_diff, 1)

            def h_split(i, a):
                dve.wait_ge(h_hi, upto(i, a))
                n = S // 2 + 1
                nc.vector.tensor_tensor(G[:, a, LO, :, 0:n], H[:, a, 1:2 * S + 5].rearrange("p (m g) -> p g m", g=4)[:, 0:3, :],
                                        G[:, a, HI, :, 0:n].bitcast(F32), ALU.subtract).then_inc(h_lo, 1)

            def r_from_psum(i, a):
                dve.wait_ge(r_psum, upto(i, a))
                if not isinstance(i, int) or i or a:
                    dve.wait_ge(r_lo, upto(i, a) - 1)
                nc.vector.tensor_scalar(R32[C:P, C:8 * C], rB[C:P, 0:7 * C], E1[C:P, bass.ds(i * 2 + a, 1)], None,
                                        ALU.mult).then_inc(r_upper, 1)
                dve.wait_ge(r_upper, upto(i, a))
                dve.wait_ge(r_lower, upto(i, a))
                r = R32[:, 0:8 * C].rearrange("p (n t c) -> p n t c", n=2, t=2)
                nc.vector.tensor_tensor(R32[:, 8 * C:12 * C].rearrange("p (n c) -> p n c", n=2), r[:, :, 0, :], r[:, :, 1, :],
                                        ALU.add).then_inc(r_sum, 1)

            def r_split(i, a):
                dve.wait_ge(r_hi, upto(i, a))
                nc.vector.tensor_tensor(RR[:, a, LO, :], R32[:], RR[:, a, HI, :].bitcast(F32), ALU.subtract).then_inc(r_lo, 1)

            def y_from_psum(i, a, first=False):
                dve.wait_ge(y_psum, upto(i, a))
                dve.wait_ge(y_mid, upto(i, a))
                if not first:
                    dve.wait_ge(yt_psum, upto(i, a) - 2)

                def shifted(t):
                    return t[:, 0:S + 2].rearrange("p (f m) -> p f m", f=2)[:, :, 0:S // 2 - 1]

                nc.vector.scalar_tensor_tensor(Y[:, a, 1:S - 1].rearrange("p (m f) -> p f m", f=2), shifted(ytB),
                                               d_all[:, 3, bass.ds(i * 2 + a, 1)], shifted(mid),
                                               ALU.mult, ALU.add).then_inc(y_out, 1)

            def yt_out(i, a, par):
                dve.wait_ge(yt_hi, upto(i, a))
                nc.vector.tensor_tensor(YT[:, par, LO, :, C * a:C * a + C], tB[:, :].rearrange("p (c o) -> p c o", o=C),
                                        YT[:, par, HI, :, C * a:C * a + C].bitcast(F32), ALU.subtract).then_inc(yt_lo, 1)

            def route(j):
                zB = fB[0]
                dve.wait_ge(z_psum, j + 1)
                nc.vector.tensor_tensor(lg[:], zB[:, 0:E], ebias[:], ALU.add).then_inc(z_chain, 1)
                dve.wait_ge(z_chain, j * 6 + 1)
                nc.vector.tensor_reduce(lg_max[:], lg[:], AX_X, ALU.max).then_inc(z_chain, 1)
                dve.wait_ge(z_chain, j * 6 + 2)
                nc.vector.scalar_tensor_tensor(sc[:], lg[:], lg_max[:, 0:1], first_w[:], ALU.is_ge, ALU.mult).then_inc(z_chain, 1)
                dve.wait_ge(z_chain, j * 6 + 3)
                nc.vector.tensor_reduce(sc_max[:], sc[:], AX_X, ALU.max).then_inc(z_chain, 1)
                dve.wait_ge(z_chain, j * 6 + 4)
                nc.vector.scalar_tensor_tensor(zm[:, :].rearrange("p (e r) -> p e r", r=R),
                                               sc[:, :].unsqueeze(2).broadcast_to([P, E, R]), sc_max[:, 0:1],
                                               zB[:, E:GA].rearrange("p (e r) -> p e r", r=R),
                                               ALU.is_equal, ALU.mult).then_inc(z_chain, 1)
                dve.wait_ge(z_chain, j * 6 + 5)
                nc.vector.tensor_copy(zm3[:, 0::2, :], zm[:, :].unsqueeze(1).broadcast_to([P, 2, ER])).then_inc(z_chain, 1)
                dve.wait_ge(z_chain, j * 6 + 6)
                nc.vector.tensor_tensor(zm3[:, 1, :], zm[:], zm3[:, 0, :].bitcast(F32), ALU.subtract).then_inc(zm_ready, 1)

            def add(j, r, par, k, first=False):
                dve.wait_ge(f_psum, j * 3 + (r + 1))
                if r == 0:
                    dve.wait_ge(xr_landed, j * 16 + 16)
                    if not first:
                        dve.wait_ge(out_stored[par], k * 16)
                n0, n = REG[r]
                lo = max(n0, GA)
                nc.vector.tensor_tensor(OUT[:, par, lo - GA:n0 + n - GA], fB[r][:, lo - n0:n],
                                        XR[:, lo - GA:n0 + n - GA], ALU.add).then_inc(added, 1)

            def step(i, par, k, conv=True, ahead=True, late=False):
                kf = k - 1 + par
                if conv:
                    q_split(i, 0)
                    if late:
                        late_bank(0)
                        late_bank(1)
                    h_from_psum(i, 0)
                    h_from_psum(i, 1)
                    h_columns(i)
                    h_differences(i, 0)
                    h_differences(i, 1)
                    h_split(i, 0)
                    if late:
                        late_bank(2)
                        late_bank(3)
                    r_from_psum(i, 0)
                    q_split(i, 1)
                    if late:
                        late_bank(4)
                    r_split(i, 0)
                    r_from_psum(i, 1)
                    h_split(i, 1)
                    y_from_psum(i, 0)
                    r_split(i, 1)
                route(i - 1)
                if conv:
                    yt_out(i, 0, par)
                    if late:
                        late_bank(5)
                    if ahead:
                        scale_t(i + 1, 0)
                        split_x(i + 1, 0)
                    y_from_psum(i, 1)
                    if ahead:
                        split_x(i + 1, 1)
                for r in range(2):
                    add(i - 1, r, 1 - par, kf, first=isinstance(i, int) and i <= 2)
                if conv:
                    yt_out(i, 1, par)
                add(i - 1, 2, 1 - par, kf)
                if conv and ahead:
                    scale_t(i + 1, 1)

            def w_bank(n0, n1):
                for n in range(n0, n1):
                    dve.wait_ge(wt_hi, n + 1)
                    if n == GA_BANK:
                        lo, hi = WT[:, LO, :, 0:GA], WT[:, HI, :, 0:GA]
                        src = fB[n % 3][:, 0:CH * GA].rearrange("p (c o) -> p c o", o=GA)
                    elif n in (GA_BANK + 1, GA_BANK + 2):
                        continue
                    else:
                        lo, hi = w_up_place(LO, half_of(n)), w_up_place(HI, half_of(n))
                        src = fB[n % 3][:, :].rearrange("p (c o) -> p c o", o=P)
                    nc.vector.tensor_tensor(lo, src, hi.bitcast(F32), ALU.subtract).then_inc(wt_lo, 1)

            def late_bank(m):
                dve.wait_ge(wt_hi, NB + m + 1)
                nc.vector.tensor_tensor(w_up_place(LO, half_of(NB + m)), fB[LATE_PLACE[m]][:, :].rearrange("p (c o) -> p c o", o=P),
                                        w_up_place(HI, half_of(NB + m)).bitcast(F32), ALU.subtract).then_inc(wt_lo, 1)

            dve.wait_ge(stat_hi, 1)
            for tabs in (slice(0, 2), slice(7, 8)):
                ins = nc.vector.tensor_tensor(stat[:, LO, tabs, :], stat32[:, tabs, :], stat[:, HI, tabs, :].bitcast(F32),
                                              ALU.subtract)
            ins.then_inc(stat_lo, 1)
            split_x(0, 0)
            split_x(0, 1)
            dve.wait_ge(wT_ready, 3)

            def blur_3(j):
                return nc.vector.scalar_tensor_tensor(V3T[:, j:j + 3, :], wT[:, 3 * K:4 * K, 0:C], BLUR[j],
                                                      V3T[:, j:j + 3, :], ALU.mult, ALU.add)

            nc.vector.scalar_tensor_tensor(rt_tmp[:], d_all[:], -0.5, d_all[:], ALU.mult, ALU.mult)
            link(blur_3(0))
            nc.vector.tensor_tensor(rt_tmp[:], rt_tmp[:], var[:], ALU.mult)
            link(blur_3(1))
            nc.vector.scalar_tensor_tensor(d_all[:], rt_tmp[:], 1.5, d_all[:], ALU.add, ALU.mult)
            link(blur_3(2))
            blur_3(3).then_inc(v3_ready, 1)
            nc.vector.scalar_tensor_tensor(E1[:], d_all[:, 0, :], SCALE, d_all[:, 1, :], ALU.mult, ALU.mult)
            nc.vector.tensor_tensor(b0d[:], var[:, 0, :], d_all[:, 0, :], ALU.mult)
            nc.vector.tensor_tensor(E2[:], s2[:], s_all[:, 1, :], ALU.mult)
            nc.vector.tensor_tensor(E3[:], s3[:], d_all[:, 2, :], ALU.mult)
            link(nc.vector.tensor_scalar(u_bias8[:], u_bias[:], BLUR[0], None, ALU.mult))
            nc.vector.tensor_scalar(b0d[:], b0d[:], smallT[:, L:L + 1], None, ALU.mult).then_inc(scales_ready, 1)
            edge_h()
            scale_t(0, 0)
            h_from_psum(0, 0)
            h_from_psum(0, 1)
            q_split(0, 0)
            scale_t(0, 1)
            w_bank(0, 2)
            edge_u()
            dve.wait_ge(h_col_ready, 1)
            h_columns(0)
            h_differences(0, 0)
            r_from_psum(0, 0)
            q_split(0, 1)
            w_bank(2, 3)
            r_split(0, 0)
            h_differences(0, 1)
            edge_v()
            w_bank(3, 4)
            r_from_psum(0, 1)
            edge_y()
            w_bank(4, 5)
            y_from_psum(0, 0, first=True)
            r_split(0, 1)
            w_bank(5, 7)
            yt_out(0, 0, 0)
            split_x(1, 0)
            w_bank(9, 10)
            split_x(1, 1)
            y_from_psum(0, 1, first=True)
            scale_t(1, 0)
            w_bank(10, 11)
            scale_t(1, 1)
            w_bank(11, NB)
            yt_out(0, 1, 0)
            dve.wait_ge(l_ga, 48)
            step(1, 1, 0, late=True)
            step(2, 0, 1)
            with dve.Fori(0, (PAIRS - 4) // 2) as k:
                step(k * 2 + 3, 1, k + 1)
                step(k * 2 + 4, 0, k + 2)
            step(PAIRS - 1, 1, PAIRS // 2 - 1, ahead=False)
            step(PAIRS, 0, PAIRS // 2, conv=False)

        @block.tensor
        def _(pe):
            pe.wait_ge(ident_ready, 1)
            pe.wait_ge(l_mod, 32)
            pe.transpose(qB[:, 0:B], cond_nat[:], ident[0:C, 0:C])
            for g in range(2):
                mm = pe.transpose(qB[:, P + P * g:2 * P + P * g], modw_nat[:, g, :], ident[:])
            mm.then_inc(modT_psum, 1)
            pe.wait_ge(l_bias, 32)
            pe.transpose(tB[:, 0:2 * L], small[:], ident[0:2 * L, 0:2 * L])
            pe.wait_ge(modT_ready, 1)
            for i in range(L):
                mm = pe.matmul(rB[:, B * i:B * i + B], modwT[:, i, :, :].rearrange("p a c -> p (a c)"), condT[:],
                               start=True, stop=True)
            mm.then_inc(s_psum, 1)

            def taps(n):
                for t in range(4):
                    mm = pe.transpose(fB[n][:, P * t:P * t + P],
                                      w_dup[:, 4 * n + t, :, :].rearrange("p a c -> p (a c)"), ident[:])
                mm.then_inc(wT_psum, 1)

            pe.wait_ge(w_dup_ready, 1)
            taps(0)
            pe.wait_ge(w2_ready, 1)
            for i in range(L):
                mm = pe.transpose(hB[0:C, P * i:P * i + P], w2_sum[:, i, :], ident[:])
            mm.then_inc(w2T_psum, 1)
            taps(1)
            pe.wait_ge(s_ready, 1)
            pe.wait_ge(w2T_ready, 1)
            for i in range(L):
                mm = pe.matmul(yB[:, B * i:B * i + B], w2_sumT[:, i, :], s_sq[0:C, i, :], start=True, stop=True)
            mm.then_inc(d_psum, 1)
            taps(2)

            def edge_h():
                pe.wait_ge(xs_edge_ready, 1)
                for side in range(EDGES):
                    for k in range(K):
                        mm = pe.matmul((tB, qB)[side][:, 0:5 * B], wT[0:C, k, :], xs_edge[:, side, k:k + 5, :],
                                       start=(k == 0), stop=(k == K - 1))
                    mm.then_inc(he_psum, 1)

            def edge_u():
                pe.wait_ge(v1n_ready, 5)
                pe.wait_ge(h_mid, 1)
                for side in range(EDGES):
                    pe.wait_ge(he_ready, side + 1)
                    for k in range(3):
                        mm = pe.matmul((tB, yB)[side][:, 0:4 * B], V1n[:, 2 * k:2 * k + 2, :].rearrange("p a c -> p (a c)"),
                                       h_edge_s[:, side, 2 - k:6 - k, :], start=(k == 0), stop=(k == 2))
                    mm.then_inc(ue_psum, 1)

            def edge_v():
                pe.wait_ge(etab_ready, 1)
                pe.wait_ge(ue_ready, 1)
                for n, at in enumerate((1, 0, 2)):
                    for side in range(EDGES):
                        pe.matmul(tB[:, 3 * B * side:3 * B * side + 3 * B], v_tab[:, n, :], u_edge[:, side, at:at + 3, :],
                                  start=(n == 0 and side == 0), stop=(n == 2), skip_group_check=True)
                    mm = pe.matmul(tB[:, 6 * B:7 * B], v_tab[:, n, :], u_bias[:], start=False, stop=(n == 2),
                                   skip_group_check=True)
                mm.then_inc(ve_psum, 1)

            def edge_y():
                pe.wait_ge(ve_ready, 1)
                pe.wait_ge(etab_ready, 2)
                for j in range(4):
                    pe.matmul(tB[:, 0:2 * B], y_tab[:, j, :], v_edge[:, :, j, :], start=(j == 0), stop=(j == 3),
                              skip_group_check=True)
                    mm = pe.matmul(tB[:, 2 * B:3 * B], y_tab[:, j, :], v_int[:], start=False, stop=(j == 3),
                                   skip_group_check=True)
                mm.then_inc(ye_psum, 1)

            PASS = ((HI, HI), (HI, LO), (LO, HI))
            FP = 3 * CH

            def conv_h(i, first=False):
                pe.wait_ge(xs_lo, upto(i, 1))
                if not first:
                    pe.wait_ge(y_out, i * 2)
                for dst, tab, g, done in ((yB, 7, 1, h_x2), (hB, 0, 0, None), (rB, 1, 2, h_psum)):
                    for n, (w, m) in enumerate(PASS):
                        mm = pe.matmul(dst[:, :], stat[:, w, tab, :], XS[:, :, m, g, :], start=(n == 0), stop=(n == 2))
                    if done:
                        mm.then_inc(done, 1)

            def make_q(i, a, first=False):
                pe.wait_ge(t_lo, upto(i, a))
                if not first or a:
                    pe.wait_ge(q_lo, upto(i, a) - 1)
                for n, (w, m) in enumerate(PASS):
                    for t in range(2):
                        mm = pe.matmul(qB[:, C * t:C * t + 4 * C], stat[:, w, 2 + t, :], TT[:, a, m, :],
                                       start=(n == 0 and t == 0), stop=(n == 2), skip_group_check=True)
                mm.then_inc(q_psum, 1)

            def make_r(i, a):
                pe.wait_ge(q_lo, upto(i, a))
                if a:
                    pe.wait_ge(r_lower, upto(i, 0))
                    pe.wait_ge(r_upper, upto(i, 0))
                else:
                    pe.wait_ge(h_out, upto(i, 1))
                for n, (w, m) in enumerate(PASS):
                    for t in range(3):
                        mm = pe.matmul(rB[:, C * t:C * t + 5 * C], stat[:, w, 4 + t, :], Q[:, m, :],
                                       start=(n == 0 and t == 0), stop=(n == 2), skip_group_check=True)
                mm.then_inc(r_psum, 1)

            def conv_y(i, a):
                pe.wait_ge(r_lo, upto(i, a))
                pe.wait_ge(h_lo, upto(i, a))
                if a:
                    pe.wait_ge(y_out, upto(i, 0))
                N = S // 2
                for dst, taps, g, done in ((hB[:, 0:N], (5, 4), 1, y_x2), (yB[:, N:S], (3, 1), 0, None),
                                           (yB[:, 0:N], (2, 0), 2, y_psum)):
                    for n, (w, m) in enumerate(PASS):
                        for t in range(2):
                            mm = pe.matmul(dst, RR[:, a, w, P * taps[t]:P * taps[t] + P], G[:, a, m, g, t:t + N],
                                           start=(n == 0 and t == 0 and g != 2), stop=(n == 2 and t == 1),
                                           skip_group_check=(g != 1))
                    if done:
                        mm.then_inc(done, 1)

            def turn_y(i, a):
                pair_0 = isinstance(i, int) and i == 0
                pe.wait_ge(y_out, upto(i, a))
                pe.wait_ge(y_cols, upto(i, a))
                if not pair_0 or a:
                    pe.wait_ge(yt_lo, upto(i, a) - 1)
                if not pair_0 and a:
                    pe.wait_ge(zt_ready, i)
                for s in range(SB):
                    mm = pe.transpose(tB[:, P * s:P * s + P], Y[:, a, P * s:P * s + P], ident[:])
                mm.then_inc(yt_psum, 1)

            def ffn(j, r, par, first_product, end, first=False):
                if first_product == 0:
                    if not first:
                        pe.wait_ge(added, j * 3 - (2 - r))
                    pe.wait_ge(yt_lo, upto(j, 1))
                n0, n = REG[r]
                for k in range(first_product, end):
                    c, (w, m) = k // 3, PASS[k % 3]
                    mm = pe.matmul(fB[r][:, 0:n], YT[:, par, w, c, :], WT[:, m, c, n0:n0 + n],
                                   start=(k == 0), stop=(k == FP - 1))
                return mm

            def turn_z(j, conv):
                pe.wait_ge(zm_ready, j + 1)
                pe.wait_ge(yt_lo, upto(j + 1, 0) if conv else upto(j, 1))
                pe.transpose(tB[0:3 * ER, 0:P], zm3[:, :, :].rearrange("p a z -> p (a z)").bitcast(F32),
                             ident[:]).then_inc(zt_psum, 1)

            def low_rank(j, r):
                n0, n = REG[r]
                lo = max(n0, GA)
                pe.matmul(fB[r][:, lo - n0:n], zT[:], BT[:, lo - GA:n0 + n - GA], start=False, stop=True,
                          skip_group_check=True).then_inc(f_psum, 1)

            def step(i, par, conv=True):
                ffn_first = isinstance(i, int) and i == 1
                j, q = i - 1, 1 - par
                if conv:
                    make_q(i, 0)
                    conv_h(i)
                if ffn_first:
                    pe.wait_ge(wt_hi, NB)
                    pe.wait_ge(wt_lo, NB - 2)
                    late_bank(0)
                    late_bank(1)
                ffn(j, 0, q, 0, FP, ffn_first).then_inc(z_psum, 1)
                if ffn_first:
                    late_bank(2)
                    late_bank(3)
                if conv:
                    make_r(i, 0)
                    make_q(i, 1)
                if ffn_first:
                    late_bank(4)
                    pe.wait_ge(wt_lo, NB - 2 + 4)
                ffn(j, 1, q, 0, FP // 2, ffn_first)
                if conv:
                    make_r(i, 1)
                    conv_y(i, 0)
                ffn(j, 1, q, FP // 2, FP, ffn_first)
                if ffn_first:
                    late_bank(5)
                if conv:
                    turn_y(i, 0)
                    conv_y(i, 1)
                turn_z(j, conv)
                if ffn_first:
                    pe.wait_ge(wt_lo, NB - 2 + LATE)
                ffn(j, 2, q, 0, FP // 2 + 1, ffn_first)
                pe.wait_ge(zt_ready, i)
                low_rank(j, 0)
                low_rank(j, 1)
                if conv:
                    turn_y(i, 1)
                ffn(j, 2, q, FP // 2 + 1, FP, ffn_first)
                low_rank(j, 2)

            def w_up_bank(h, dst):
                ob = h // 2
                pe.wait_ge(l_wup[ob % 3], 16 * (ob // 3 + 1))
                for t in range(CH // 2):
                    c = CH // 2 * (h % 2) + t
                    t0 = 2 * P * (c // 2) + c % 2
                    mm = pe.transpose(dst[:, P * t:P * t + P], wup_nat[:, ob % 3, t0:t0 + 2 * P - 1:2], ident[:])
                return mm

            def w_bank(n0, n1):
                for n in range(n0, n1):
                    if n - 3 in (GA_BANK + 1, GA_BANK + 2):
                        pe.wait_ge(wt_hi, n - 2)
                    elif n >= 3:
                        pe.wait_ge(wt_lo, n - 2 - (0 if n - 3 <= GA_BANK else 2))
                    if n == GA_BANK:
                        pe.wait_ge(l_ga, 48)
                        for c in range(CH):
                            t0 = 2 * P * (c // 2) + c % 2
                            mm = pe.transpose(fB[n % 3][:, GA * c:GA * c + GA], ga_nat[:, t0:t0 + 2 * P - 1:2],
                                              ident[0:GA, 0:GA])
                    elif n in (GA_BANK + 1, GA_BANK + 2):
                        pe.wait_ge(lb3_ready, 1)
                        for t in range(4):
                            g = 4 * (n - GA_BANK - 1) + t
                            mm = pe.transpose(fB[n % 3][0:3 * ER, P * t:P * t + P],
                                              lb3[:, g, :, :].rearrange("p a z -> p (a z)").bitcast(F32), ident[:])
                    else:
                        mm = w_up_bank(half_of(n), fB[n % 3])
                    mm.then_inc(wt_psum, 1)

            def late_bank(m):
                before = [k for k in range(m) if LATE_PLACE[k] == LATE_PLACE[m]]
                if before:
                    pe.wait_ge(wt_lo, NB - 2 + before[-1] + 1)
                w_up_bank(half_of(NB + m), fB[LATE_PLACE[m]]).then_inc(wt_psum, 1)

            pe.wait_ge(wT_ready, 3)
            w_bank(0, 3)
            edge_h()
            pe.wait_ge(stat_lo, 1)
            conv_h(0, True)
            pe.wait_ge(stat_lo_qr, 1)
            pe.wait_ge(he_ready, 2)
            make_q(0, 0, True)
            edge_u()
            make_r(0, 0)
            make_q(0, 1)
            w_bank(3, 4)
            edge_v()
            make_r(0, 1)
            conv_y(0, 0)
            edge_y()
            w_bank(4, 7)
            pe.wait_ge(edges_ready, 1)
            turn_y(0, 0)
            w_bank(7, 10)
            conv_y(0, 1)
            w_bank(10, NB)
            turn_y(0, 1)
            step(1, 1)
            with pe.Fori(0, (PAIRS - 2) // 2) as k:
                step(k * 2 + 2, 0)
                step(k * 2 + 3, 1)
            step(PAIRS, 0, conv=False)


_INS = ["x", "cond_512", "L0_cond_weights", "L0_cond_biases", "L0_cond_mod_w", "L0_cond_mod_b", "L0_ffn_W_up",
        "L0_ffn_gate_w", "L0_ffn_expert_bias", "L0_ffn_lora_A", "L0_ffn_lora_B"]


def kernel(**inputs):
    import numpy as _np
    import concourse.bacc as _bacc
    from concourse import mybir as _mybir
    from concourse.bass_utils import run_bass_kernel_spmd as _run

    nc = _bacc.Bacc("TRN2", target_bir_lowering=False, num_devices=1)
    arrays, args = {}, []
    for name in _INS:
        a = _np.ascontiguousarray(inputs[name])
        arrays[f"in_{name}_dram"] = a
        args.append(nc.dram_tensor(f"in_{name}_dram", a.shape, _mybir.dt.from_np(a.dtype), kind="ExternalInput").ap())
    out = nc.dram_tensor("out_dram", inputs["x"].shape, _mybir.dt.float32, kind="ExternalOutput").ap()
    adaln_ffn_kernel(nc, *args, out)
    r = _run(nc, [arrays], core_ids=[0])
    return r.results[0]["out_dram"]
```
